# Optimizing a Trainium2 kernel written in Bass

```python
import numpy as np
import jax
import jax.numpy as jnp

def _softmax(x, axis=-1):
    return jax.nn.softmax(x, axis=axis)

def _gelu(x):
    return jax.nn.gelu(x, approximate=True)

def _silu(x):
    return jax.nn.silu(x)

def _sigmoid(x):
    return jax.nn.sigmoid(x)

def _layernorm(x, axis=-1, eps=1e-05):
    m = jnp.mean(x, axis=axis, keepdims=True)
    v = jnp.var(x, axis=axis, keepdims=True)
    return (x - m) / jnp.sqrt(v + eps)

def _scatter_add(tgt, idx, src, axis=0):
    return tgt.at[idx].add(src)

def _segment_sum(src, seg, n):
    return jax.ops.segment_sum(src, seg, n)
kernel_name = 'mk_xattn_ffn_d1_seqx_r8_9b7b0c'

def setup_inputs(seed: int=0):
    np.random.seed(seed)
    _w = jnp.asarray

    def _rec_inputs():
        import jax
        import jax.numpy as jnp
        _rk = jax.random.key(seed)
        x = -0.0002928 + 1 * jax.random.normal(jax.random.fold_in(_rk, 1), (64, 64, 128), jnp.float32)
        _lenS = 64 - jax.random.randint(jax.random.fold_in(_rk, 7), (64,), 0, max(1, 64 // 4) + 1, jnp.int32)
        _lenS2 = 64 - jax.random.randint(jax.random.fold_in(_rk, 8), (64,), 0, max(1, 64 // 4) + 1, jnp.int32)
        _ctx_1024P = jax.random.normal(jax.random.fold_in(_rk, 11), (64, 16, 128), jnp.float32)
        _ctx_1024c = jax.random.dirichlet(jax.random.fold_in(_rk, 511), 0.3 * jnp.ones((16,), jnp.float32), (64, 64))
        _ctx_1024t = jnp.einsum('bsk,bkd->bsd', _ctx_1024c, _ctx_1024P)
        _ctx_1024t = _ctx_1024t * jax.lax.rsqrt(jnp.mean(jnp.square(_ctx_1024t)) + 1e-12) * 0.953939
        ctx_1024 = -1.39393e-06 + 0.999914 * (_ctx_1024t + 0.3 * jax.random.normal(jax.random.fold_in(_rk, 611), (64, 64, 128), jnp.float32))
        _validS = jnp.arange(64)[None, :] < _lenS[:, None]
        _validS2 = jnp.arange(64)[None, :] < _lenS2[:, None]
        _causal = jnp.tril(jnp.ones((64, 64), dtype=bool))
        mask_BxS2_bf1 = jnp.ones((64, 64), dtype=bool)
        return (x, ctx_1024, mask_BxS2_bf1)
    x, ctx_1024, mask_BxS2_bf1 = _rec_inputs()

    def _L0_xattn_setup():
        import jax, jax.numpy as jnp
        import numpy as np
        N_HEADS = 16
        HEAD_DIM = 64
        EMB = 128
        B, S = (2, 256)
        key = jax.random.key(seed)
        ks = jax.random.split(key, 8)
        inner = N_HEADS * HEAD_DIM
        return {'query': jax.random.normal(ks[0], (B, S, EMB), dtype=jnp.float32), 'key': jax.random.normal(ks[1], (B, S, EMB), dtype=jnp.float32), 'value': jax.random.normal(ks[2], (B, S, EMB), dtype=jnp.float32), 'positional_mask': jnp.ones((B, S), dtype=bool), 'future_mask': 1, 'Wq': jax.random.normal(ks[3], (inner, EMB), dtype=jnp.float32) * 0.02, 'Wk': jax.random.normal(ks[4], (inner, EMB), dtype=jnp.float32) * 0.02, 'Wv': jax.random.normal(ks[5], (inner, EMB), dtype=jnp.float32) * 0.02, 'Wo': jax.random.normal(ks[6], (EMB, inner), dtype=jnp.float32) * 0.02, 'bo': jax.random.normal(ks[7], (EMB,), dtype=jnp.float32) * 0.02}
    _L0_xattn_all = _L0_xattn_setup()
    _L0_xattn_in = {k: v for k, v in _L0_xattn_all.items() if k in ('Wq', 'Wk', 'Wv', 'Wo', 'bo')}
    del _L0_xattn_all

    def _L0_ffn_setup():
        import jax, jax.numpy as jnp
        import numpy as np
        H = 128
        M = 64
        E = 16
        TOP_K = 2
        SCALE = 2.5
        NORM_TOPK = True
        B, S = (1, 128)

        def _moe(x, gate_w, w_gate, w_up, w_down, ws_gate, ws_up, ws_down):
            T = x.shape[0]
            shared = jax.nn.silu(x @ ws_gate) * (x @ ws_up) @ ws_down
            scores = jax.nn.sigmoid(x.astype(jnp.float32) @ gate_w.T.astype(jnp.float32))
            topk_w, topk_idx = jax.lax.top_k(scores, TOP_K)
            if NORM_TOPK and TOP_K > 1:
                topk_w = topk_w / (topk_w.sum(-1, keepdims=True) + 1e-20)
            topk_w = topk_w * SCALE
            route = jnp.zeros((T, E), topk_w.dtype).at[jnp.arange(T)[:, None], topk_idx].set(topk_w)
            g = jnp.einsum('th,ehm->etm', x, w_gate)
            u = jnp.einsum('th,ehm->etm', x, w_up)
            eo = jnp.einsum('etm,emh->eth', jax.nn.silu(g) * u, w_down)
            routed = jnp.einsum('te,eth->th', route.astype(x.dtype), eo)
            return routed + shared
        key = jax.random.key(seed)
        ks = jax.random.split(key, 8)
        std = 0.02
        return {'hidden_states': jax.random.normal(ks[0], (B, S, H), jnp.float32), 'gate_w': jax.random.normal(ks[1], (E, H), jnp.float32) * std, 'w_gate': jax.random.normal(ks[2], (E, H, M), jnp.float32) * std, 'w_up': jax.random.normal(ks[3], (E, H, M), jnp.float32) * std, 'w_down': jax.random.normal(ks[4], (E, M, H), jnp.float32) * std, 'ws_gate': jax.random.normal(ks[5], (H, M), jnp.float32) * std, 'ws_up': jax.random.normal(ks[6], (H, M), jnp.float32) * std, 'ws_down': jax.random.normal(ks[7], (M, H), jnp.float32) * std}
    _L0_ffn_all = _L0_ffn_setup()
    _L0_ffn_in = {k: v for k, v in _L0_ffn_all.items() if k in ('gate_w', 'w_gate', 'w_up', 'w_down', 'ws_gate', 'ws_up', 'ws_down')}
    del _L0_ffn_all
    return {'x': x, 'ctx_1024': ctx_1024, 'mask_BxS2_bf1': mask_BxS2_bf1, 'L0_xattn_Wq': _L0_xattn_in['Wq'], 'L0_xattn_Wk': _L0_xattn_in['Wk'], 'L0_xattn_Wv': _L0_xattn_in['Wv'], 'L0_xattn_Wo': _L0_xattn_in['Wo'], 'L0_xattn_bo': _L0_xattn_in['bo'], 'L0_ffn_gate_w': _L0_ffn_in['gate_w'], 'L0_ffn_w_gate': _L0_ffn_in['w_gate'], 'L0_ffn_w_up': _L0_ffn_in['w_up'], 'L0_ffn_w_down': _L0_ffn_in['w_down'], 'L0_ffn_ws_gate': _L0_ffn_in['ws_gate'], 'L0_ffn_ws_up': _L0_ffn_in['ws_up'], 'L0_ffn_ws_down': _L0_ffn_in['ws_down']}

def reference(x, ctx_1024, mask_BxS2_bf1, L0_xattn_Wq, L0_xattn_Wk, L0_xattn_Wv, L0_xattn_Wo, L0_xattn_bo, L0_ffn_gate_w, L0_ffn_w_gate, L0_ffn_w_up, L0_ffn_w_down, L0_ffn_ws_gate, L0_ffn_ws_up, L0_ffn_ws_down):
    import jax
    import jax.numpy as jnp

    def _L0_xattn_ref(query, key, value, positional_mask, future_mask, Wq, Wk, Wv, Wo, bo):
        import jax, jax.numpy as jnp
        import numpy as np
        N_HEADS = 16
        HEAD_DIM = 64
        EMB = 128
        B, S = (2, 256)
        batch, seq = query.shape[:2]
        q = (query @ Wq.T).reshape(batch, seq, N_HEADS, HEAD_DIM)
        k = (key @ Wk.T).reshape(batch, seq, N_HEADS, HEAD_DIM)
        v = (value @ Wv.T).reshape(batch, seq, N_HEADS, HEAD_DIM)
        scale = 1.0 / np.sqrt(HEAD_DIM).astype(np.float32)
        weights = jnp.einsum('bqhd,bkhd->bhqk', q, k) * scale
        neg_inf = jnp.float32(-jnp.inf)
        reweight = jnp.where(positional_mask, jnp.float32(0.0), neg_inf)
        weights = weights + reweight[:, None, None, :]
        if future_mask:
            causal = jnp.triu(jnp.full((seq, seq), neg_inf, dtype=weights.dtype), k=1)
            weights = weights + causal
        weights = jax.nn.softmax(weights, axis=-1)
        out = jnp.einsum('bhqk,bkhd->bqhd', weights, v).reshape(batch, seq, -1)
        return out @ Wo.T + bo

    def _L0_ffn_ref(hidden_states, gate_w, w_gate, w_up, w_down, ws_gate, ws_up, ws_down):
        import jax, jax.numpy as jnp
        import numpy as np
        H = 128
        M = 64
        E = 16
        TOP_K = 2
        SCALE = 2.5
        NORM_TOPK = True
        B, S = (1, 128)

        def _moe(x, gate_w, w_gate, w_up, w_down, ws_gate, ws_up, ws_down):
            T = x.shape[0]
            shared = jax.nn.silu(x @ ws_gate) * (x @ ws_up) @ ws_down
            scores = jax.nn.sigmoid(x.astype(jnp.float32) @ gate_w.T.astype(jnp.float32))
            topk_w, topk_idx = jax.lax.top_k(scores, TOP_K)
            if NORM_TOPK and TOP_K > 1:
                topk_w = topk_w / (topk_w.sum(-1, keepdims=True) + 1e-20)
            topk_w = topk_w * SCALE
            route = jnp.zeros((T, E), topk_w.dtype).at[jnp.arange(T)[:, None], topk_idx].set(topk_w)
            g = jnp.einsum('th,ehm->etm', x, w_gate)
            u = jnp.einsum('th,ehm->etm', x, w_up)
            eo = jnp.einsum('etm,emh->eth', jax.nn.silu(g) * u, w_down)
            routed = jnp.einsum('te,eth->th', route.astype(x.dtype), eo)
            return routed + shared
        b, s, h = hidden_states.shape
        x = hidden_states.reshape(-1, h)
        out = _moe(x, gate_w, w_gate, w_up, w_down, ws_gate, ws_up, ws_down)
        return out.reshape(b, s, h)
    x = x + _L0_xattn_ref(_layernorm(x, axis=-1), ctx_1024, ctx_1024, mask_BxS2_bf1, 1, L0_xattn_Wq, L0_xattn_Wk, L0_xattn_Wv, L0_xattn_Wo, L0_xattn_bo)
    x = x + _L0_ffn_ref(_layernorm(x, axis=-1), L0_ffn_gate_w, L0_ffn_w_gate, L0_ffn_w_up, L0_ffn_w_down, L0_ffn_ws_gate, L0_ffn_ws_up, L0_ffn_ws_down)
    return x

_drawn_inputs = setup_inputs


def setup_inputs(seed=0):
    import zlib

    import numpy as np

    out = dict(_drawn_inputs(seed))
    spreads = {}
    factors = {'L0_xattn_Wq': 8.0,
     'L0_xattn_Wk': 8.0,
     'L0_xattn_bo': 2.676,
     'L0_ffn_gate_w': 8.0,
     'L0_ffn_w_gate': 7.746,
     'L0_ffn_w_up': 7.73,
     'L0_ffn_w_down': 7.694,
     'L0_ffn_ws_gate': 8.0,
     'L0_ffn_ws_up': 8.0,
     'L0_ffn_ws_down': 8.0}
    for name, (base, spread) in spreads.items():
        noise = np.random.default_rng([zlib.crc32(name.encode()), seed]).standard_normal(out[name].shape)
        drawn = base * np.exp(spread * noise) if base else spread * noise
        out[name] = jnp.asarray(drawn.astype(out[name].dtype))
    for name, factor in factors.items():
        out[name] = (out[name] * factor).astype(out[name].dtype)
    return out
```

```python
from contextlib import ExitStack

import concourse.bass as bass
from concourse import mybir

F32 = mybir.dt.float32
F32R = mybir.dt.float32r
BF16 = mybir.dt.bfloat16
ALU = mybir.AluOpType
ACT = mybir.ActivationFunctionType
AX_X = mybir.AxisListType.X

P = 128
HEADS = 16
HD = 64
SEQ = 64
EXPERTS = 16
MID = 64
TOP_SCALE = 2.5
LN_EPS = 1e-5
SATURATED = 20.0
MASKED = -1e30


def at_least(eng, sem, value):
    if isinstance(value, int) and value <= 0:
        return
    eng.wait_ge(sem, value)


def xattn_moe_kernel(nc, x, ctx_in, mask, Wq, Wk, Wv, Wo, bo, gate_w, w_gate, w_up, w_down,
                     ws_gate, ws_up, ws_down, out):
    batches = x.shape[0]
    PAIRS = batches // 2
    BODIES = PAIRS // 4
    GROUPS = PAIRS // 2
    GT = 2 * P
    BLOCKS = EXPERTS // 2 + 1
    QUADS = PAIRS // 4
    QT = 4 * P

    x_tiles = x.rearrange("(t b) s d -> (t b s) d", b=2).rearrange("(t p) d -> p t d", p=P)
    out_tiles = out.rearrange("(t b) s d -> (t b s) d", b=2).rearrange("(t p) d -> p t d", p=P)

    with ExitStack() as stack:
        def sb(name, shape, dt=F32):
            return stack.enter_context(nc.sbuf_tensor(name, shape, dt))

        def sem(name):
            return stack.enter_context(nc.semaphore(name))

        bank = [stack.enter_context(nc.psum_tensor(f"bank{i}", [P, 512], F32)) for i in range(8)]
        rot = bank[0:3]
        score_bank = bank[3:5]
        pv_bank = bank[5:7]
        acc = bank[7]

        xall = sb("xall", [P, PAIRS, P])
        keys = sb("keys", [P, 2, HEADS, GT])
        r_hi = sb("r_hi", [P, 2, HEADS, GT], F32R)
        r_lo = sb("r_lo", [P, 2, HEADS, GT], F32R)
        pt_hi = sb("pt_hi", [P, 8, P], F32R)
        pt_lo = sb("pt_lo", [P, 8, P], F32R)
        probs = sb("probs", [P, HEADS, SEQ])
        craw = sb("craw", [P, 2, 4, P])
        c_hi = sb("c_hi", [P, 2, 4, P], F32R)
        c_lo = sb("c_lo", [P, 2, 4, P], F32R)
        ct_hi = sb("ct_hi", [P, GT], F32R)
        ct_lo = sb("ct_lo", [P, GT], F32R)
        xt = sb("xt", [P, 2, GT])
        xn = sb("xn", [P, 2, P])
        attn_t = sb("attn_t", [P, GT])
        m_hi = sb("m_hi", [P, HEADS, P], F32R)
        m_lo = sb("m_lo", [P, HEADS, P], F32R)
        b_hi = sb("b_hi", [P, HEADS, P], F32R)
        b_lo = sb("b_lo", [P, HEADS, P], F32R)
        wg_hi = sb("wg_hi", [P, BLOCKS, P], F32R)
        wg_lo = sb("wg_lo", [P, BLOCKS, P], F32R)
        wu_hi = sb("wu_hi", [P, BLOCKS - 1, P], F32R)
        wu_lo = sb("wu_lo", [P, BLOCKS - 1, P], F32R)
        maskb = sb("maskb", [P, PAIRS, SEQ], BF16)
        tri = sb("tri", [P, SEQ])
        ident = sb("ident", [P, P])
        ident_b = sb("ident_b", [P, P], BF16)
        mask_u8 = sb("mask_u8", [2, PAIRS, SEQ], mask.dtype)
        half_of = sb("half_of", [2, P], BF16)
        bo_col = sb("bo_col", [P, 1])
        gw_row = sb("gw_row", [EXPERTS, P])
        gw_t = sb("gw_t", [P, EXPERTS])
        wait_cell = sb("wait_cell", [P, 1])
        zero_col = sb("zero_col", [P, 1])
        stats = sb("stats", [P, 4, 6])
        mean_var = sb("mean_var", [P, 4, 2])
        var_eps = sb("var_eps", [P, 4, 1])
        rstd = sb("rstd", [P, 4, 1])
        minus_half = sb("minus_half", [P, 4, 1])
        row_max = sb("row_max", [P, HEADS])
        row_sum = sb("row_sum", [P, HEADS])
        nan_probe = sb("nan_probe", [P, HEADS])
        inv_raw = sb("inv_raw", [P, HEADS])
        inv = sb("inv", [P, HEADS])
        logit_fix = sb("logit_fix", [P, 4, EXPERTS])
        logit = sb("logit", [P, 4, EXPERTS])
        logit_inv = sb("logit_inv", [P, 4, EXPERTS])
        logit_silu = sb("logit_silu", [P, 4, EXPERTS])
        score = sb("score", [P, 4, EXPERTS + 8])
        best = sb("best", [P, 4, 8])
        taken = sb("taken", [P, 4, 8])
        marked = sb("marked", [P, 4, EXPERTS + 8])
        best_sum = sb("best_sum", [P, 4, 1])
        best_inv = sb("best_inv", [P, 4, 1])
        picked = sb("picked", [P, 4, EXPERTS])
        route = sb("route", [P, 4, EXPERTS])
        route2 = sb("route2", [P, 4, 2 * EXPERTS], F32R)

        keys_flat = keys[:].rearrange("p a h t -> p (a h t)")
        wq_s = keys_flat[0:HD, 0:2048].rearrange("p (h e) -> p h e", h=HEADS)
        wk_s = keys_flat[0:HD, 2048:4096].rearrange("p (h e) -> p h e", h=HEADS)
        wv_s = keys_flat[0:HD, 4096:6144].rearrange("p (h e) -> p h e", h=HEADS)
        wo_t = keys_flat[0:HD, 6144:8192].rearrange("p (h e) -> p h e", h=HEADS)
        mask_neg = keys_flat[0:2, 0:1024].bitcast(BF16).rearrange("b (t k) -> b t k", k=SEQ)
        sel_f = keys_flat[0:2 * EXPERTS, 4096:5120].rearrange("p (n r) -> p n r", n=8)
        sel = pt_lo[0:2 * EXPERTS]
        route_t = pt_hi[0:2 * EXPERTS, 0:4, :].rearrange("p n t -> p (n t)")
        wo_s = probs[:].rearrange("p h k -> p (h k)")
        wg_raw = keys_flat[:, 0:1152]
        wu_raw = keys_flat[:, 1152:2176]
        wd_raw = keys_flat[:, 2176:3328]
        sg = keys_flat[:, 4096:5632].rearrange("p (n t) -> p n t", n=3)
        hid = keys_flat[:, 5632:7168].rearrange("p (n t) -> p n t", n=3)
        y_t = keys_flat[:, 7168:7680]
        out_sb = keys_flat[:, 7680:8192].rearrange("p (n d) -> p n d", n=4)
        wd_hi = m_hi[:, 0:BLOCKS, :]
        wd_lo = m_lo[:, 0:BLOCKS, :]
        rh_flat = r_hi[:].rearrange("p a h t -> p (a h t)")
        rl_flat = r_lo[:].rearrange("p a h t -> p (a h t)")
        x2_hi = rh_flat[:, 0:4096].rearrange("p (g t) -> p g t", g=QUADS)
        x2_lo = rl_flat[:, 0:4096].rearrange("p (g t) -> p g t", g=QUADS)
        hid_hi = rh_flat[:, 4096:5632].rearrange("p (n t) -> p n t", n=3)
        hid_lo = rl_flat[:, 4096:5632].rearrange("p (n t) -> p n t", n=3)
        probs_flat = probs[:].rearrange("p h k -> p (h k)")
        x2_f = probs_flat[:, 0:QT]
        xn2 = probs_flat[:, QT:2 * QT].rearrange("p (n d) -> p n d", n=4)

        wk_in, wo_in, x_first_in, x_rest_in = sem("wk_in"), sem("wo_in"), sem("x_first_in"), sem("x_rest_in")
        wv_in, mask_in, small_in, ffn_in = sem("wv_in"), sem("mask_in"), sem("small_in"), sem("ffn_in")
        ctx_landed = [sem("ctx_even_in"), sem("ctx_odd_in")]
        pool_step, consts_made = sem("pool_step"), sem("consts_made")
        sel_made, mask_neg_made = sem("sel_made"), sem("mask_neg_made")
        m_done, m_hi_made, m_lo_made = sem("m_done"), sem("m_hi_made"), sem("m_lo_made")
        wot_done, wot_copied = sem("wot_done"), sem("wot_copied")
        b_done, b_hi_made, b_lo_made = sem("b_done"), sem("b_hi_made"), sem("b_lo_made")
        mask_spread, mask_made = sem("mask_spread"), sem("mask_made")
        ctx_hi_made, ctx_lo_made = sem("ctx_hi_made"), sem("ctx_lo_made")
        ct_done, ct_hi_made, ct_lo_made = sem("ct_done"), sem("ct_hi_made"), sem("ct_lo_made")
        keys_done, keys_copied = sem("keys_done"), sem("keys_copied")
        ln_step, var_made, rstd_made = sem("ln_step"), sem("var_made"), sem("rstd_made")
        xn_made, xt_done, xt_copied = sem("xn_made"), sem("xt_done"), sem("xt_copied")
        scores_done, max_made, shifted, exp_made = sem("scores_done"), sem("max_made"), sem("shifted"), sem("exp_made")
        sum_made, inv_step, inv_made, probs_made = sem("sum_made"), sem("inv_step"), sem("inv_made"), sem("probs_made")
        pt_done, pt_hi_made, pt_lo_made = sem("pt_done"), sem("pt_hi_made"), sem("pt_lo_made")
        pv_done, r_hi_made, r_lo_made = sem("pv_done"), sem("r_hi_made"), sem("r_lo_made")
        attn_done, attn_copied, attn_turned, x2_made = sem("attn_done"), sem("attn_copied"), sem("attn_turned"), sem("x2_made")
        ffn_hi_made, ffn_lo_made = sem("ffn_hi_made"), sem("ffn_lo_made")
        gwt_done, gwt_copied = sem("gwt_done"), sem("gwt_copied")
        ln2_step, var2_made, rstd2_made = sem("ln2_step"), sem("var2_made"), sem("rstd2_made")
        xn2_made, x2t_done = sem("xn2_made"), sem("x2t_done")
        x2_hi_made, x2_f_made, x2_lo_made = sem("x2_hi_made"), sem("x2_f_made"), sem("x2_lo_made")
        logit_done, logit_step, logit_made, silu_of_logit = sem("logit_done"), sem("logit_step"), sem("logit_made"), sem("silu_of_logit")
        top_step, route_made, route_turned, route_copied = sem("top_step"), sem("route_made"), sem("route_turned"), sem("route_copied")
        fill_made, route_step = sem("fill_made"), sem("route_step")
        gate_done, up_done, silu_made, hid_made = sem("gate_done"), sem("up_done"), sem("silu_made"), sem("hid_made")
        prod_made, hid_hi_made, hid_lo_made = sem("prod_made"), sem("hid_hi_made"), sem("hid_lo_made")
        y_done, y_copied, y_turned, out_made, out_stored = sem("y_done"), sem("y_copied"), sem("y_turned"), sem("out_made"), sem("out_stored")

        block = stack.enter_context(nc.Block())

        def once(bank_):
            return bank_[:].rearrange("p (b a k) -> p b a k", a=2, k=SEQ)[:, :, 0, :]

        @block.sync
        def _(sp):
            def load_ctx(group, parity):
                for half in range(2):
                    sp.dma_start(craw[half * SEQ:(half + 1) * SEQ, parity],
                                 ctx_in[bass.ds(4 * group, 4)].rearrange("b k e -> k b e")
                                 ).then_inc(ctx_landed[parity], 16)

            sp.dma_start(wq_s, Wq.rearrange("(h d) e -> d h e", d=HD)).then_inc(wk_in, 16)
            sp.dma_start(wk_s, Wk.rearrange("(h d) e -> d h e", d=HD)).then_inc(wk_in, 16)
            sp.dma_start(wo_s, Wo).then_inc(wo_in, 16)
            sp.dma_start(wv_s, Wv.rearrange("(h d) e -> d h e", d=HD)).then_inc(wv_in, 16)
            load_ctx(0, 0)
            sp.dma_start(xall[:, 0:4, :], x_tiles[:, 0:4, :]).then_inc(x_first_in, 16)
            load_ctx(1, 1)
            sp.dma_start(mask_u8[:], mask.rearrange("(t b) k -> b t k", b=2)).then_inc(mask_in, 16)
            sp.dma_start(bo_col[:], bo.rearrange("(d a) -> d a", a=1)).then_inc(small_in, 16)
            sp.dma_start(gw_row[:], gate_w).then_inc(small_in, 16)
            sp.dma_start(xall[:, 4:PAIRS, :], x_tiles[:, 4:PAIRS, :]).then_inc(x_rest_in, 16)

            def body(i, last):
                for parity in range(2):
                    if last:
                        continue
                    group = 2 * i + parity
                    sp.wait_ge(ctx_lo_made, group + 1)
                    sp.wait_ge(ct_done, group + 1)
                    load_ctx(group + 2, parity)

            with sp.Fori(0, BODIES - 1) as i:
                body(i, False)

            sp.wait_ge(scores_done, 2 * (PAIRS - 2))
            sp.dma_start(wg_raw[:, 0:1024].rearrange("p (e m) -> p e m", m=MID),
                         w_gate.rearrange("e h m -> h e m")).then_inc(ffn_in, 16)
            sp.dma_start(wg_raw[:, 1024:1088], ws_gate).then_inc(ffn_in, 16)
            sp.dma_start(wg_raw[:, 1088:1152], ws_up).then_inc(ffn_in, 16)
            sp.dma_start(wu_raw.rearrange("p (e m) -> p e m", m=MID),
                         w_up.rearrange("e h m -> h e m")).then_inc(ffn_in, 16)
            sp.dma_start(wd_raw[:, 0:1024].rearrange("p (n d) -> p n d", d=P),
                         w_down.rearrange("(n a) m d -> (a m) n d", a=2)).then_inc(ffn_in, 16)
            sp.dma_start(wd_raw[0:MID, 1024:1152], ws_down).then_inc(ffn_in, 16)

            with sp.Fori(0, QUADS) as quad:
                sp.wait_ge(out_made, quad + 1)
                sp.dma_start(out_tiles[:, bass.ds(4 * quad, 4), :], out_sb).then_inc(out_stored, 16)
            sp.wait_ge(out_stored, 16 * QUADS)

        @block.gpsimd
        def _(pool):
            steps = [0]

            def step(ins):
                steps[0] += 1
                ins.then_inc(pool_step, 1)
                pool.wait_ge(pool_step, steps[0])

            step(nc.gpsimd.memset(ident[:], 0.0))
            step(nc.gpsimd.affine_select(out=ident[:], in_=ident[:], compare_op=ALU.not_equal, fill=1.0,
                                         base=0, pattern=[[-1, P]], channel_multiplier=1))
            nc.gpsimd.tensor_copy(ident_b[:], ident[:]).then_inc(consts_made, 1)
            step(nc.gpsimd.memset(tri[:], 0.0))
            for half in range(2):
                rows = tri[half * SEQ:(half + 1) * SEQ, :]
                nc.gpsimd.affine_select(out=rows, in_=rows, compare_op=ALU.is_ge, fill=MASKED, base=0,
                                        pattern=[[-1, SEQ]], channel_multiplier=1).then_inc(consts_made, 1)
            step(nc.gpsimd.memset(half_of[:], 1.0))
            step(nc.gpsimd.affine_select(out=half_of[:], in_=half_of[:], compare_op=ALU.is_ge, fill=0.0,
                                         base=0, pattern=[[1, P]], channel_multiplier=-SEQ))
            nc.gpsimd.affine_select(out=half_of[:], in_=half_of[:], compare_op=ALU.is_ge, fill=0.0,
                                    base=SEQ - 1, pattern=[[-1, P]], channel_multiplier=SEQ).then_inc(consts_made, 1)

            def split_ctx(group, parity, round_):
                at_least(pool, pv_done, 8 * (group - 1))
                pool.wait_ge(ctx_landed[parity], 32 * (round_ + 1))
                nc.gpsimd.tensor_tensor(c_hi[:, parity], craw[:, parity],
                                        zero_col[:].unsqueeze(1).to_broadcast([P, 4, P]), ALU.add
                                        ).then_inc(ctx_hi_made, 1)
                pool.wait_ge(ctx_hi_made, group + 1)
                nc.gpsimd.tensor_tensor(c_lo[:, parity], craw[:, parity], c_hi[:, parity],
                                        ALU.subtract).then_inc(ctx_lo_made, 1)

            def normalise(pair):
                pool.wait_ge(inv_made, pair + 1)
                for half in range(2):
                    heads = slice(8 * half, 8 * half + 8)
                    nc.gpsimd.tensor_tensor(probs[:, heads, :], probs[:, heads, :],
                                            inv[:, heads].unsqueeze(2).to_broadcast([P, 8, SEQ]),
                                            ALU.mult).then_inc(probs_made, 1)

            nc.gpsimd.memset(minus_half[:], -0.5).then_inc(fill_made, 1)
            nc.gpsimd.memset(zero_col[:], 0.0).then_inc(fill_made, 1)
            pool.wait_ge(fill_made, 2)

            def deviation(group, n, made, done):
                pool.wait_ge(made, group + 1)
                nc.gpsimd.tensor_tensor(rstd[:, 0:n, :], var_eps[:, 0:n, :], minus_half[:, 0:n, :], ALU.pow
                                        ).then_inc(done, 1)

            deviation(0, 2, var_made, rstd_made)
            split_ctx(0, 0, 0)
            deviation(1, 2, var_made, rstd_made)
            split_ctx(1, 1, 0)
            nc.gpsimd.memset(score[:], -1.0).then_inc(fill_made, 1)
            nc.gpsimd.memset(taken[:], -1.0).then_inc(fill_made, 1)
            normalise(0)

            def body(i, last):
                for s in range(4):
                    pair, parity = 4 * i + s, s // 2
                    if s % 2 == 1 and not last:
                        deviation(2 * i + parity + 2, 2, var_made, rstd_made)
                    if not (last and s == 3):
                        normalise(pair + 1)
                    if s % 2 == 1 and not last:
                        split_ctx(2 * i + parity + 2, parity, i + 1)

            with pool.Fori(0, BODIES - 1) as i:
                body(i, False)
            body(BODIES - 1, True)

            pool.wait_ge(scores_done, 2 * PAIRS)
            step(nc.gpsimd.memset(sel_f, 0.0))
            for first_row in (0, EXPERTS):
                ins = nc.gpsimd.affine_select(out=sel_f, in_=sel_f, compare_op=ALU.not_equal, fill=1.0,
                                              base=-first_row, pattern=[[-2, 8], [-1, 2], [0, MID]],
                                              channel_multiplier=1)
                step(ins)
            pool.wait_ge(pv_done, 4 * PAIRS)
            nc.gpsimd.tensor_copy(sel, sel_f).then_inc(sel_made, 1)

            def x2_low(quad):
                pool.wait_ge(x2_f_made, quad + 1)
                nc.gpsimd.tensor_tensor(x2_lo[:, bass.ds(quad, 1), :].rearrange("p a t -> p (a t)"), x2_f,
                                        x2_hi[:, bass.ds(quad, 1), :].rearrange("p a t -> p (a t)"),
                                        ALU.subtract).then_inc(x2_lo_made, 1)

            def hid_low(quad, n):
                rows = P if n < BLOCKS - 1 else MID
                step_no = BLOCKS * quad + n
                pool.wait_ge(hid_hi_made, step_no + 1)
                nc.gpsimd.tensor_tensor(hid_lo[0:rows, n % 3], hid[0:rows, n % 3], hid_hi[0:rows, n % 3],
                                        ALU.subtract).then_inc(hid_lo_made, 1)

            def quad_body(quad, last):
                for n in range(BLOCKS):
                    if n == 0 and not last:
                        deviation(quad + 1, 4, var2_made, rstd2_made)
                    hid_low(quad, n)
                    if n == 3 and not last:
                        x2_low(quad + 1)

            deviation(0, 4, var2_made, rstd2_made)
            x2_low(0)
            with pool.Fori(0, QUADS - 1) as quad:
                quad_body(quad, False)
            quad_body(QUADS - 1, True)

        @block.tensor
        def _(pe):
            def three(out_, a_hi, a_lo, b_hi_, b_lo_, start=True, stop=True):
                nc.tensor.matmul(out_, a_hi, b_hi_, start=start, stop=False)
                nc.tensor.matmul(out_, a_lo, b_hi_, start=False, stop=False)
                return nc.tensor.matmul(out_, a_hi, b_lo_, start=False, stop=stop)

            pe.wait_ge(wk_in, 32)
            for c in range(4):
                for j in range(4):
                    h = 4 * c + j
                    last = nc.tensor.matmul(bank[c][:, j * P:(j + 1) * P], wk_s[:, h, :], wq_s[:, h, :],
                                            start=True, stop=True)
                last.then_inc(m_done, 1)
            pe.wait_ge(wo_in, 16)
            pe.wait_ge(consts_made, 4)
            for c in range(4):
                for j in range(4):
                    h = 4 * c + j
                    last = nc.tensor.transpose(bank[4 + c][0:HD, j * P:(j + 1) * P],
                                               wo_s[:, h * HD:(h + 1) * HD], ident[:])
                last.then_inc(wot_done, 1)
            pe.wait_ge(wv_in, 16)
            for c in range(4):
                pe.wait_ge(m_lo_made, c + 1)
                pe.wait_ge(wot_copied, c + 1)
                for j in range(4):
                    h = 4 * c + j
                    last = nc.tensor.matmul(bank[c][:, j * P:(j + 1) * P], wv_s[:, h, :], wo_t[:, h, :],
                                            start=True, stop=True)
                last.then_inc(b_done, 1)
            pe.wait_ge(mask_neg_made, 1)
            for c in range(4):
                nc.tensor.matmul(bank[4 + c][:], half_of[:],
                                 mask_neg.rearrange("b t k -> b (t k)")[:, 512 * c:512 * c + 512],
                                 start=True, stop=True).then_inc(mask_spread, 1)
            pe.wait_ge(b_lo_made, 4)
            pe.wait_ge(mask_made, 4)

            def turn_ctx(group, parity, round_):
                pe.wait_ge(ctx_landed[parity], 32 * (round_ + 1))
                for b in range(4):
                    last = nc.tensor.transpose(rot[1][:, b * P:(b + 1) * P], craw[:, parity, b, :], ident[:])
                last.then_inc(ct_done, 1)

            def turn_x(group, into):
                pe.wait_ge(xn_made, group + 1)
                for k in range(2):
                    last = nc.tensor.transpose(into[:, k * P:(k + 1) * P], xn[:, k, :], ident[:])
                last.then_inc(xt_done, 1)

            def project_keys(j, into):
                for a in range(2):
                    h = 2 * j + a
                    last = three(into[:, a * GT:(a + 1) * GT], m_hi[:, h, :], m_lo[:, h, :], ct_hi[:], ct_lo[:])
                last.then_inc(keys_done, 1)

            def scores(pair, s):
                parity, r = s // 2, s % 2
                group = (pair - r) // 2 if isinstance(pair, int) else None
                for half in range(2):
                    at_least(pe, shifted, 2 * (pair - 1) + half + 1)
                    seen = maskb[:, bass.ds(pair, 1), :].to_broadcast([P, 8, SEQ])
                    nc.tensor.matmul(score_bank[half][:], ident_b[:], seen, start=True, stop=False,
                                     skip_group_check=True)
                    for b in range(2):
                        col = r * P + b * SEQ
                        last = nc.tensor.matmul(score_bank[half][b * SEQ:(b + 1) * SEQ, :],
                                                xt[:, parity, col:col + SEQ],
                                                keys[:, parity, 8 * half:8 * half + 8, col:col + SEQ],
                                                start=False, stop=True, skip_group_check=True)
                    last.then_inc(scores_done, 1)

            def turn_probs(pair, v, into):
                pe.wait_ge(probs_made, 2 * pair + v + 1)
                for k in range(4):
                    src = probs[:, 8 * v + 2 * k:8 * v + 2 * k + 2, :].rearrange("p h k -> p (h k)")
                    last = nc.tensor.transpose(into[:, k * P:(k + 1) * P], src, ident[:])
                last.then_inc(pt_done, 1)

            def probs_by_ctx(pair, s, b):
                parity, r = s // 2, s % 2
                for part in range(3):
                    w = c_lo if part == 1 else c_hi
                    m = pt_lo if part == 2 else pt_hi
                    for h2 in range(2):
                        if part == 0:
                            at_least(pe, r_lo_made, 4 * pair + 2 * b + h2 - 1)
                        rows = slice(h2 * SEQ, (h2 + 1) * SEQ)
                        last = nc.tensor.matmul(pv_bank[h2][:], w[rows, parity, 2 * r + b, :],
                                                m[rows, :, b * SEQ:(b + 1) * SEQ],
                                                start=(part == 0), stop=(part == 2))
                        if part == 2:
                            last.then_inc(pv_done, 1)

            def add_heads(group, parity, heads):
                for h in heads:
                    last = three(acc[:, 0:GT], b_hi[:, h, :], b_lo[:, h, :], r_hi[:, parity, h, :],
                                 r_lo[:, parity, h, :], start=(h == 0), stop=(h == HEADS - 1))
                if heads[-1] == HEADS - 1:
                    last.then_inc(attn_done, 1)

            def turn_attn(group, into):
                pe.wait_ge(attn_copied, group + 1)
                for k in range(2):
                    last = nc.tensor.transpose(into[:, k * P:(k + 1) * P], attn_t[:, k * P:(k + 1) * P], ident[:])
                last.then_inc(attn_turned, 1)

            turn_ctx(0, 0, 0)
            turn_x(0, rot[0])
            pe.wait_ge(ct_lo_made, 1)
            for j in range(8):
                if j == 1:
                    pe.wait_ge(xt_copied, 1)
                if j == 2:
                    pe.wait_ge(ct_lo_made, 1)
                at_least(pe, keys_copied, j - 2)
                project_keys(j, rot[(j + 2) % 3])
            pe.wait_ge(keys_copied, 6)
            turn_ctx(1, 1, 0)
            pe.wait_ge(ct_lo_made, 2)
            project_keys(0, rot[1])
            pe.wait_ge(keys_copied, 7)
            project_keys(1, rot[2])
            pe.wait_ge(keys_copied, 8)
            project_keys(2, rot[0])
            scores(0, 0)
            pe.wait_ge(keys_copied, 9)
            project_keys(3, rot[1])

            def body(i, first, last):
                for s in range(4):
                    pair, parity, r = 4 * i + s, s // 2, s % 2
                    group = 2 * i + parity
                    last_group = last and parity == 1
                    if not (last and s == 3):
                        if r == 0:
                            at_least(pe, keys_copied, 8 * group + 8)
                        else:
                            pe.wait_ge(xt_copied, group + 2)
                            pe.wait_ge(keys_copied, 8 * (group + 1) + 8)
                        scores(pair + 1, (s + 1) % 4)
                    at_least(pe, pt_lo_made, 2 * pair)
                    if r == 0:
                        if not last_group:
                            pe.wait_ge(keys_copied, 8 * (group + 1) + 3)
                        turn_probs(pair, 0, rot[0])
                        if not last_group:
                            pe.wait_ge(keys_copied, 8 * (group + 1) + 4)
                        turn_probs(pair, 1, rot[1])
                    else:
                        if not last_group:
                            pe.wait_ge(keys_copied, 8 * (group + 1) + 8)
                        else:
                            at_least(pe, x2_made, group - 2)
                        turn_probs(pair, 0, rot[2])
                        if not last_group:
                            pe.wait_ge(xt_copied, group + 2)
                        turn_probs(pair, 1, rot[0])
                    if r == 0 and not last_group:
                        at_least(pe, r_lo_made, 4 * pair - 2)
                        project_keys(4, rot[2])
                        pe.wait_ge(pt_lo_made, 2 * pair + 1)
                        project_keys(5, rot[0])
                        pe.wait_ge(pt_lo_made, 2 * pair + 2)
                        project_keys(6, rot[1])
                        pe.wait_ge(keys_copied, 8 * (group + 1) + 5)
                        project_keys(7, rot[2])
                        pe.wait_ge(keys_copied, 8 * (group + 1) + 6)
                        turn_x(group + 1, rot[0])
                        if not last:
                            pe.wait_ge(keys_copied, 8 * (group + 1) + 7)
                            turn_ctx(group + 2, parity, i + 1)
                    if r == 1 and not last:
                        pe.wait_ge(ct_lo_made, group + 3)
                        project_keys(0, rot[1])
                        pe.wait_ge(pt_lo_made, 2 * pair + 1)
                        project_keys(1, rot[2])
                        pe.wait_ge(pt_lo_made, 2 * pair + 2)
                        project_keys(2, rot[0])
                        pe.wait_ge(keys_copied, 8 * (group + 2) + 1)
                        project_keys(3, rot[1])
                    if r == 1 and not first:
                        pe.wait_ge(keys_copied, 8 * (group + 2) + 2) if not last else pe.wait_ge(pt_lo_made, 2 * pair + 1)
                        turn_attn(group - 2, rot[2])
                    pe.wait_ge(pt_lo_made, 2 * pair + 2)
                    if r == 0:
                        pe.wait_ge(ctx_lo_made, group + 1)
                    for b in range(2):
                        probs_by_ctx(pair, s, b)
                        if first and parity == 0:
                            continue
                        if r == 0 and b == 0:
                            pe.wait_ge(r_lo_made, 8 * group)
                            at_least(pe, attn_copied, group - 1)
                        k = 8 * r + 4 * b
                        add_heads(group - 1, 1 - parity, range(k, k + 4))

            body(0, True, False)
            with pe.Fori(1, BODIES - 1) as i:
                body(i, False, False)
            body(BODIES - 1, False, True)
            pe.wait_ge(r_lo_made, 4 * PAIRS)
            pe.wait_ge(attn_copied, GROUPS - 1)
            pe.wait_ge(pt_lo_made, 2 * PAIRS)
            add_heads(GROUPS - 1, 1, range(0, 8))
            turn_attn(GROUPS - 2, rot[0])
            add_heads(GROUPS - 1, 1, range(8, HEADS))
            turn_attn(GROUPS - 1, rot[1])

            gate_bank, up_bank, spread_bank, misc = bank[0:2], bank[2:4], bank[4:6], bank[6]

            pe.wait_ge(small_in, 32)
            nc.tensor.transpose(misc[:, 0:EXPERTS], gw_row[:], ident[0:EXPERTS, 0:EXPERTS]).then_inc(gwt_done, 1)
            pe.wait_ge(gwt_copied, 1)
            pe.wait_ge(x2_made, GROUPS)

            def turn_x2(quad):
                at_least(pe, out_made, quad - 1)
                pe.wait_ge(xn2_made, quad + 1)
                for k in range(4):
                    last = nc.tensor.transpose(misc[:, k * P:(k + 1) * P], xn2[:, k, :], ident[:])
                last.then_inc(x2t_done, 1)

            def logits(quad):
                pe.wait_ge(x2_f_made, quad + 1)
                for k in range(4):
                    last = nc.tensor.matmul(misc[:, k * EXPERTS:(k + 1) * EXPERTS], x2_f[:, k * P:(k + 1) * P],
                                            gw_t[:], start=True, stop=True)
                last.then_inc(logit_done, 1)

            def turn_route(quad):
                pe.wait_ge(route_made, quad + 1)
                for k in range(4):
                    last = nc.tensor.transpose(misc[0:2 * EXPERTS, k * P:(k + 1) * P],
                                               route2[:, k, :].bitcast(F32), ident[:])
                last.then_inc(route_turned, 1)

            def up(quad, n):
                hi = x2_hi[:, bass.ds(quad, 1), :].rearrange("p a t -> p (a t)")
                lo = x2_lo[:, bass.ds(quad, 1), :].rearrange("p a t -> p (a t)")
                q = n % 2
                step_no = BLOCKS * quad + n
                at_least(pe, prod_made, step_no if n == 0 else step_no - 1)
                three(gate_bank[q][:], wg_hi[:, n, :], wg_lo[:, n, :], hi, lo).then_inc(gate_done, 1)
                if n == BLOCKS - 1:
                    return
                three(up_bank[q][:], wu_hi[:, n, :], wu_lo[:, n, :], hi, lo)
                if n == 0:
                    pe.wait_ge(route_copied, quad + 1)
                at_least(pe, hid_made, 8 * quad + n - 1)
                nc.tensor.matmul(spread_bank[q][:], sel[:, n, :], route_t, start=True, stop=True
                                 ).then_inc(up_done, 1)

            def down(quad, n):
                rows = P if n < BLOCKS - 1 else MID
                if n == 0:
                    at_least(pe, y_copied, quad)
                pe.wait_ge(hid_lo_made, BLOCKS * quad + n + 1)
                last = three(acc[:], wd_hi[0:rows, n, :], wd_lo[0:rows, n, :], hid_hi[0:rows, n % 3],
                             hid_lo[0:rows, n % 3], start=(n == 0), stop=(n == BLOCKS - 1))
                if n == BLOCKS - 1:
                    last.then_inc(y_done, 1)

            def quad_body(quad, first, last):
                for n in range(BLOCKS):
                    if n == BLOCKS - 1 and not last:
                        turn_route(quad + 1)
                    if n == 0:
                        pe.wait_ge(x2_lo_made, quad + 1)
                    up(quad, n)
                    if n >= 2:
                        down(quad, n - 2)
                    elif not first:
                        down(quad - 1, BLOCKS - 2 + n)
                    if n == 2 and not first:
                        turn_y_of_last(quad)
                    if n == 3 and not last:
                        turn_x2(quad + 1)
                    if n == 5 and not last:
                        logits(quad + 1)

            def turn_y_of_last(quad):
                pe.wait_ge(y_copied, quad)
                pe.wait_ge(route_copied, quad + 1)
                for k in range(4):
                    last = nc.tensor.transpose(misc[:, k * P:(k + 1) * P], y_t[:, k * P:(k + 1) * P], ident[:])
                last.then_inc(y_turned, 1)

            turn_x2(0)
            logits(0)
            pe.wait_ge(ffn_lo_made, 4)
            turn_route(0)
            quad_body(0, True, False)
            with pe.Fori(1, QUADS - 1) as quad:
                quad_body(quad, False, False)
            quad_body(QUADS - 1, False, True)
            down(QUADS - 1, BLOCKS - 2)
            down(QUADS - 1, BLOCKS - 1)
            pe.wait_ge(y_copied, QUADS)
            pe.wait_ge(out_made, QUADS - 1)
            for k in range(4):
                last_turn = nc.tensor.transpose(misc[:, k * P:(k + 1) * P], y_t[:, k * P:(k + 1) * P], ident[:])
            last_turn.then_inc(y_turned, 1)

        @block.scalar
        def _(act):
            copy = lambda dst, src: nc.scalar.activation(dst, src, ACT.Copy)

            for c in range(4):
                act.wait_ge(m_done, c + 1)
                copy(m_hi[:, 4 * c:4 * c + 4, :].rearrange("p h e -> p (h e)"), bank[c][:]).then_inc(m_hi_made, 1)
            for c in range(4):
                act.wait_ge(wot_done, c + 1)
                copy(wo_t[:, 4 * c:4 * c + 4, :].rearrange("p h e -> p (h e)"),
                     bank[4 + c][0:HD, :]).then_inc(wot_copied, 1)
            for c in range(4):
                act.wait_ge(b_done, c + 1)
                copy(b_hi[:, 4 * c:4 * c + 4, :].rearrange("p h e -> p (h e)"), bank[c][:]).then_inc(b_hi_made, 1)

            def ctx_t_high(group):
                act.wait_ge(ct_done, group + 1)
                copy(ct_hi[:].rearrange("p (b k) -> p b k", k=SEQ), once(rot[1])).then_inc(ct_hi_made, 1)

            def x_t(group, parity, src):
                act.wait_ge(xt_done, group + 1)
                at_least(act, scores_done, 4 * (group - 1))
                copy(xt[:, parity, :], src[:, 0:GT]).then_inc(xt_copied, 1)

            def keys_out(group, parity, j, src):
                act.wait_ge(keys_done, 8 * group + j + 1)
                if j == 0:
                    at_least(act, scores_done, 4 * (group - 1))
                copy(keys[:, parity, 2 * j:2 * j + 2, :].rearrange("p h t -> p (h t)"), src[:]
                     ).then_inc(keys_copied, 1)

            def exponentials(pair, half):
                act.wait_ge(shifted, 2 * pair + half + 1)
                part = probs[:, 8 * half:8 * half + 8, :]
                nc.scalar.activation(part, part, ACT.Exp, scale=HD ** -0.5).then_inc(exp_made, 1)

            def probs_t_high(pair, v, src):
                act.wait_ge(pt_done, 2 * pair + v + 1)
                if v == 0:
                    at_least(act, pv_done, 4 * pair)
                copy(pt_hi[:, 4 * v:4 * v + 4, :].rearrange("p h q -> p (h q)"), src[:]).then_inc(pt_hi_made, 1)

            def r_high(pair, s, b):
                parity, r = s // 2, s % 2
                for h2 in range(2):
                    act.wait_ge(pv_done, 4 * pair + 2 * b + h2 + 1)
                    col = r * P + b * SEQ
                    dst = r_hi[:, parity, :, col:col + SEQ].rearrange("p (n a) q -> p n a q", a=2)[:, :, h2, :]
                    copy(dst, pv_bank[h2][:].rearrange("p (n q) -> p n q", q=SEQ)).then_inc(r_hi_made, 1)

            def attn_out(group):
                act.wait_ge(attn_done, group + 1)
                at_least(act, attn_turned, group)
                nc.scalar.activation(attn_t[:], acc[:, 0:GT], ACT.Identity, bias=bo_col[:, 0:1]
                                     ).then_inc(attn_copied, 1)

            ctx_t_high(0)
            x_t(0, 0, rot[0])
            for j in range(8):
                keys_out(0, 0, j, rot[(j + 2) % 3])
            ctx_t_high(1)
            for j in range(4):
                keys_out(1, 1, j, rot[(j + 1) % 3])
            exponentials(0, 0)
            exponentials(0, 1)
            act.wait_ge(small_in, 32)

            def body(i, first, last):
                for s in range(4):
                    pair, parity, r = 4 * i + s, s // 2, s % 2
                    group = 2 * i + parity
                    last_group = last and parity == 1
                    if r == 0 and not (first and parity == 0) and not (first and parity == 1):
                        attn_out(group - 2)
                    turned = (rot[0], rot[1]) if r == 0 else (rot[2], rot[0])
                    probs_t_high(pair, 0, turned[0])
                    probs_t_high(pair, 1, turned[1])
                    have_keys = not last_group if r == 0 else not last
                    key_args = ([(group + 1, 1 - parity, 4 + j, rot[(j + 2) % 3]) for j in range(4)] if r == 0 else
                                [(group + 2, parity, j, rot[(j + 1) % 3]) for j in range(4)])
                    for j in range(4):
                        if have_keys:
                            keys_out(*key_args[j])
                        if j in (1, 2) and not (last and s == 3):
                            exponentials(pair + 1, j - 1)
                    if r == 0 and not last_group:
                        x_t(group + 1, 1 - parity, rot[0])
                        if not last:
                            ctx_t_high(group + 2)
                    r_high(pair, s, 0)
                    r_high(pair, s, 1)

            body(0, True, False)
            with act.Fori(1, BODIES - 1) as i:
                body(i, False, False)
            body(BODIES - 1, False, True)
            attn_out(GROUPS - 2)
            attn_out(GROUPS - 1)

            act.wait_ge(gwt_done, 1)
            copy(gw_t[:], bank[6][:, 0:EXPERTS]).then_inc(gwt_copied, 1)
            gate_bank, misc = bank[0:2], bank[6]

            def x2_high(quad):
                act.wait_ge(x2t_done, quad + 1)
                copy(x2_hi[:, bass.ds(quad, 1), :].rearrange("p a t -> p (a t)"), misc[:]).then_inc(x2_hi_made, 1)
                copy(x2_f, misc[:]).then_inc(x2_f_made, 1)

            def logit_silus(quad):
                act.wait_ge(logit_made, quad + 1)
                nc.scalar.activation(logit_silu[:], logit[:], ACT.Silu).then_inc(silu_of_logit, 1)

            def route_out(quad):
                act.wait_ge(route_turned, quad + 1)
                copy(route_t, misc[0:2 * EXPERTS, :]).then_inc(route_copied, 1)

            def silu(quad, n):
                step_no = BLOCKS * quad + n
                rows = P if n < BLOCKS - 1 else MID
                act.wait_ge(gate_done, step_no + 1)
                at_least(act, prod_made, step_no - 2)
                nc.scalar.activation(sg[0:rows, n % 3], gate_bank[n % 2][0:rows, :], ACT.Silu
                                     ).then_inc(silu_made, 1)

            def hid_high(quad, n):
                step_no = BLOCKS * quad + n
                if n < BLOCKS - 1:
                    rows = P
                    act.wait_ge(hid_made, 8 * quad + n + 1)
                else:
                    rows = MID
                    act.wait_ge(prod_made, step_no + 1)
                copy(hid_hi[0:rows, n % 3], hid[0:rows, n % 3]).then_inc(hid_hi_made, 1)

            def y_out(quad):
                act.wait_ge(y_done, quad + 1)
                copy(y_t, acc[:]).then_inc(y_copied, 1)

            def quad_body(quad, first, last):
                for n in range(BLOCKS):
                    silu(quad, n)
                    if n > 0:
                        hid_high(quad, n - 1)
                    elif not first:
                        hid_high(quad - 1, BLOCKS - 1)
                    if n == 1 and not first:
                        y_out(quad - 1)
                    if n == 3 and not last:
                        x2_high(quad + 1)
                    if n == 6 and not last:
                        logit_silus(quad + 1)
                    if n == BLOCKS - 1 and not last:
                        route_out(quad + 1)

            x2_high(0)
            logit_silus(0)
            route_out(0)
            quad_body(0, True, False)
            with act.Fori(1, QUADS - 1) as quad:
                quad_body(quad, False, False)
            quad_body(QUADS - 1, False, True)
            hid_high(QUADS - 1, BLOCKS - 1)
            y_out(QUADS - 1)

        @block.vector
        def _(dve):
            sub = lambda dst, a, b: nc.vector.tensor_tensor(dst, a, b, ALU.subtract)
            flat = lambda ap: ap.rearrange("p a b -> p (a b)")

            dve.wait_ge(mask_in, 16)
            dve.wait_ge(m_done, 4)
            nc.vector.tensor_scalar(mask_neg, mask_u8[:], -1.0, -MASKED, ALU.add, ALU.mult
                                    ).then_inc(mask_neg_made, 1)

            def wait_before(sem_, value):
                dve.wait_ge(sem_, value)
                nc.vector.memset(wait_cell[:], 0.0)

            def statistics(group):
                for k in range(2):
                    tile = flat(xall[:, bass.ds(2 * group + k, 1), :])
                    last = nc.vector.bn_stats(stats[:, k, :], tile)
                last.then_inc(ln_step, 1)
                wait_before(ln_step, 2 * group + 1)
                for k in range(2):
                    last = nc.vector.bn_aggr(mean_var[:, k, :], stats[:, k, :])
                last.then_inc(ln_step, 1)
                dve.wait_ge(ln_step, 2 * group + 2)
                nc.vector.tensor_scalar(var_eps[:, 0:2, :], mean_var[:, 0:2, 1:2], LN_EPS, None, ALU.add
                                        ).then_inc(var_made, 1)

            def layer_norm(group):
                dve.wait_ge(rstd_made, group + 1)
                at_least(dve, xt_done, group)
                for k in range(2):
                    tile = flat(xall[:, bass.ds(2 * group + k, 1), :])
                    last = nc.vector.tensor_scalar(xn[:, k, :], tile, mean_var[:, k, 0:1], rstd[:, k, :],
                                                   ALU.subtract, ALU.mult)
                last.then_inc(xn_made, 1)

            dve.wait_ge(x_first_in, 16)
            statistics(0)
            layer_norm(0)
            for c in range(4):
                dve.wait_ge(m_hi_made, c + 1)
                part = slice(4 * c, 4 * c + 4)
                sub(flat(m_lo[:, part, :]), bank[c][:], flat(m_hi[:, part, :])).then_inc(m_lo_made, 1)
            for c in range(4):
                dve.wait_ge(b_hi_made, c + 1)
                part = slice(4 * c, 4 * c + 4)
                sub(flat(b_lo[:, part, :]), bank[c][:], flat(b_hi[:, part, :])).then_inc(b_lo_made, 1)
            dve.wait_ge(consts_made, 4)
            for c in range(4):
                dve.wait_ge(mask_spread, c + 1)
                nc.vector.tensor_tensor(maskb[:, 8 * c:8 * c + 8, :],
                                        bank[4 + c][:].rearrange("p (t k) -> p t k", k=SEQ),
                                        tri[:].unsqueeze(1).to_broadcast([P, 8, SEQ]), ALU.add
                                        ).then_inc(mask_made, 1)

            def ctx_t_low(group):
                dve.wait_ge(ct_hi_made, group + 1)
                sub(ct_lo[:].rearrange("p (b k) -> p b k", k=SEQ), once(rot[1]),
                    ct_hi[:].rearrange("p (b k) -> p b k", k=SEQ)).then_inc(ct_lo_made, 1)

            def maximum(pair, half):
                dve.wait_ge(scores_done, 2 * pair + half + 1)
                nc.vector.tensor_reduce(row_max[:, 8 * half:8 * half + 8],
                                        score_bank[half][:].rearrange("p (h k) -> p h k", k=SEQ), AX_X, ALU.max
                                        ).then_inc(max_made, 1)

            def shift(pair, half):
                heads = slice(8 * half, 8 * half + 8)
                dve.wait_ge(max_made, 2 * pair + half + 1)
                if half == 0:
                    at_least(dve, pt_done, 2 * pair)
                sub(probs[:, heads, :], score_bank[half][:].rearrange("p (h k) -> p h k", k=SEQ),
                    row_max[:, heads].unsqueeze(2).to_broadcast([P, 8, SEQ])).then_inc(shifted, 1)

            def sums(pair):
                for half in range(2):
                    heads = slice(8 * half, 8 * half + 8)
                    dve.wait_ge(exp_made, 2 * pair + half + 1)
                    nc.vector.tensor_reduce(row_sum[:, heads], probs[:, heads, :], AX_X, ALU.add
                                            ).then_inc(sum_made, 1)
                nc.vector.tensor_scalar(nan_probe[:], row_max[:], 1e9, None, ALU.mult).then_inc(inv_step, 1)
                dve.wait_ge(sum_made, 2 * pair + 2)
                nc.vector.reciprocal(inv_raw[:], row_sum[:]).then_inc(inv_step, 1)
                dve.wait_ge(inv_step, 2 * pair + 2)
                at_least(dve, probs_made, 2 * pair)
                nc.vector.scalar_tensor_tensor(inv[:], nan_probe[:], 0.0, inv_raw[:], ALU.mult, ALU.add
                                               ).then_inc(inv_made, 1)

            def probs_t_low(pair, v, src):
                dve.wait_ge(pt_hi_made, 2 * pair + v + 1)
                part = slice(4 * v, 4 * v + 4)
                sub(flat(pt_lo[:, part, :]), src[:], flat(pt_hi[:, part, :])).then_inc(pt_lo_made, 1)

            def r_low(pair, s, b):
                parity, r = s // 2, s % 2
                col = r * P + b * SEQ
                for h2 in range(2):
                    dve.wait_ge(r_hi_made, 4 * pair + 2 * b + h2 + 1)
                    pick = lambda t: t[:, parity, :, col:col + SEQ].rearrange("p (n a) q -> p n a q", a=2)[:, :, h2, :]
                    sub(pick(r_lo), pv_bank[h2][:].rearrange("p (n q) -> p n q", q=SEQ), pick(r_hi)
                        ).then_inc(r_lo_made, 1)

            def add_attn(group, src):
                dve.wait_ge(attn_turned, group + 1)
                tiles = xall[:, bass.ds(2 * group, 2), :]
                nc.vector.tensor_tensor(tiles, src[:, 0:GT].rearrange("p (t d) -> p t d", d=P), tiles, ALU.add
                                        ).then_inc(x2_made, 1)

            ctx_t_low(0)
            statistics(1)
            layer_norm(1)
            ctx_t_low(1)
            for half in range(2):
                maximum(0, half)
                shift(0, half)
            sums(0)
            dve.wait_ge(x_rest_in, 16)

            def body(i, first, last):
                for s in range(4):
                    pair, parity, r = 4 * i + s, s // 2, s % 2
                    group = 2 * i + parity
                    more = not (last and s == 3)
                    if more:
                        maximum(pair + 1, 0)
                        maximum(pair + 1, 1)
                    turned = (rot[0], rot[1]) if r == 0 else (rot[2], rot[0])
                    probs_t_low(pair, 0, turned[0])
                    probs_t_low(pair, 1, turned[1])
                    if more:
                        shift(pair + 1, 0)
                        shift(pair + 1, 1)
                        sums(pair + 1)
                    if r == 0 and not last:
                        ctx_t_low(group + 2)
                    if r == 1 and not first:
                        add_attn(group - 2, rot[2])
                    r_low(pair, s, 0)
                    if r == 1 and not last:
                        layer_norm(group + 2)
                    r_low(pair, s, 1)
                    if r == 0 and not last:
                        statistics(group + 2)

            body(0, True, False)
            with dve.Fori(1, BODIES - 1) as i:
                body(i, False, False)
            body(BODIES - 1, False, True)

            up_bank, spread_bank, misc = bank[2:4], bank[4:6], bank[6]
            dve.wait_ge(ffn_in, 16 * 6)
            wu_flat = lambda t: t[:].rearrange("p n d -> p (n d)")
            parts = [(wu_flat(wg_hi), wu_flat(wg_lo), wg_raw), (wu_flat(wu_hi), wu_flat(wu_lo), wu_raw),
                     (flat(wd_hi[:, 0:8, :]), flat(wd_lo[:, 0:8, :]), wd_raw[:, 0:1024]),
                     (wd_hi[0:MID, 8, :], wd_lo[0:MID, 8, :], wd_raw[0:MID, 1024:1152])]
            add_attn(GROUPS - 2, rot[0])
            for hi, lo, raw in parts:
                nc.vector.tensor_copy(hi, raw).then_inc(ffn_hi_made, 1)
            for k, (hi, lo, raw) in enumerate(parts):
                dve.wait_ge(ffn_hi_made, k + 1)
                sub(lo, raw, hi).then_inc(ffn_lo_made, 1)
            add_attn(GROUPS - 1, rot[1])
            dve.wait_ge(x2_made, GROUPS)
            dve.wait_ge(fill_made, 4)
            dve.wait_ge(sel_made, 1)

            def statistics2(quad):
                for k in range(4):
                    last = nc.vector.bn_stats(stats[:, k, :], flat(xall[:, bass.ds(4 * quad + k, 1), :]))
                last.then_inc(ln2_step, 1)
                wait_before(ln2_step, 2 * quad + 1)
                for k in range(4):
                    last = nc.vector.bn_aggr(mean_var[:, k, :], stats[:, k, :])
                last.then_inc(ln2_step, 1)
                dve.wait_ge(ln2_step, 2 * quad + 2)
                nc.vector.tensor_scalar(var_eps[:], mean_var[:, :, 1:2], LN_EPS, None, ALU.add
                                        ).then_inc(var2_made, 1)

            def layer_norm2(quad):
                dve.wait_ge(rstd2_made, quad + 1)
                at_least(dve, x2t_done, quad)
                for k in range(4):
                    last = nc.vector.tensor_scalar(xn2[:, k, :], flat(xall[:, bass.ds(4 * quad + k, 1), :]),
                                                   mean_var[:, k, 0:1], rstd[:, k, :], ALU.subtract, ALU.mult)
                last.then_inc(xn2_made, 1)

            def fix_logits(quad):
                z = misc[:, 0:4 * EXPERTS].rearrange("p (t e) -> p t e", e=EXPERTS)
                dve.wait_ge(logit_done, quad + 1)
                nc.vector.tensor_scalar(logit_fix[:], z, 0.0, 1e-20, ALU.is_equal, ALU.mult).then_inc(logit_step, 1)
                dve.wait_ge(logit_step, 2 * quad + 1)
                at_least(dve, silu_of_logit, quad)
                nc.vector.scalar_tensor_tensor(logit[:], z, SATURATED, logit_fix[:], ALU.min, ALU.add
                                               ).then_inc(logit_made, 1)
                dve.wait_ge(logit_made, quad + 1)
                nc.vector.reciprocal(logit_inv[:], logit[:]).then_inc(logit_step, 1)

            def pick_experts(quad):
                t0 = 8 * quad
                dve.wait_ge(silu_of_logit, quad + 1)
                dve.wait_ge(logit_step, 2 * quad + 2)
                real = score[:, :, 0:EXPERTS]
                nc.vector.tensor_tensor(real, logit_silu[:], logit_inv[:], ALU.mult).then_inc(top_step, 1)
                wait_before(top_step, t0 + 1)
                for k in range(4):
                    last = nc.vector.max(best[:, k, :], score[:, k, :])
                last.then_inc(top_step, 1)
                dve.wait_ge(top_step, t0 + 2)
                nc.vector.tensor_copy(taken[:, :, 0:2], best[:, :, 0:2]).then_inc(top_step, 1)
                nc.vector.tensor_tensor(best_sum[:], best[:, :, 0:1], best[:, :, 1:2], ALU.add).then_inc(top_step, 1)
                wait_before(top_step, t0 + 4)
                for k in range(4):
                    last = nc.vector.match_replace(marked[:, k, :], taken[:, k, :], score[:, k, :], -5.0)
                last.then_inc(top_step, 1)
                nc.vector.tensor_scalar(best_sum[:], best_sum[:], 1e-20, None, ALU.add).then_inc(top_step, 1)
                dve.wait_ge(top_step, t0 + 6)
                nc.vector.reciprocal(best_inv[:], best_sum[:]).then_inc(top_step, 1)
                nc.vector.scalar_tensor_tensor(picked[:], marked[:, :, 0:EXPERTS], -3.0, real, ALU.is_lt, ALU.mult
                                               ).then_inc(top_step, 1)
                dve.wait_ge(top_step, t0 + 8)

            def split_route(quad):
                nc.vector.scalar_tensor_tensor(route[:], picked[:], TOP_SCALE,
                                               best_inv[:].to_broadcast([P, 4, EXPERTS]), ALU.mult, ALU.mult
                                               ).then_inc(route_step, 1)
                dve.wait_ge(route_step, 2 * quad + 1)
                at_least(dve, route_turned, quad)
                nc.vector.tensor_copy(route2[:, :, 0:EXPERTS], route[:]).then_inc(route_step, 1)
                dve.wait_ge(route_step, 2 * quad + 2)
                sub(route2[:, :, EXPERTS:2 * EXPERTS], route[:], route2[:, :, 0:EXPERTS]).then_inc(route_made, 1)

            def product(quad, n):
                step_no = BLOCKS * quad + n
                dve.wait_ge(silu_made, step_no + 1)
                at_least(dve, hid_lo_made, step_no - 2)
                if n < BLOCKS - 1:
                    dve.wait_ge(up_done, 8 * quad + n + 1)
                    nc.vector.tensor_tensor(hid[:, n % 3], up_bank[n % 2][:], sg[:, n % 3], ALU.mult
                                            ).then_inc(prod_made, 1)
                    dve.wait_ge(prod_made, step_no + 1)
                    nc.vector.tensor_tensor(hid[:, n % 3], spread_bank[n % 2][:], hid[:, n % 3], ALU.mult
                                            ).then_inc(hid_made, 1)
                else:
                    nc.vector.tensor_tensor(hid[0:MID, n % 3], bank[n % 2][MID:P, :], sg[0:MID, n % 3], ALU.mult
                                            ).then_inc(prod_made, 1)

            def add_experts(quad):
                dve.wait_ge(y_turned, quad + 1)
                at_least(dve, out_stored, 16 * quad)
                nc.vector.tensor_tensor(out_sb, misc[:].rearrange("p (t d) -> p t d", d=P),
                                        xall[:, bass.ds(4 * quad, 4), :], ALU.add).then_inc(out_made, 1)

            def quad_body(quad, first, last):
                for n in range(BLOCKS):
                    product(quad, n)
                    if n == 0 and not last:
                        statistics2(quad + 1)
                    if n == 1 and not last:
                        layer_norm2(quad + 1)
                    if n == 2 and not first:
                        add_experts(quad - 1)
                    if n == 5 and not last:
                        fix_logits(quad + 1)
                    if n == 6 and not last:
                        pick_experts(quad + 1)
                        split_route(quad + 1)

            statistics2(0)
            layer_norm2(0)
            fix_logits(0)
            pick_experts(0)
            split_route(0)
            quad_body(0, True, False)
            with dve.Fori(1, QUADS - 1) as quad:
                quad_body(quad, False, False)
            quad_body(QUADS - 1, False, True)
            add_experts(QUADS - 1)


_INS = ['x', 'ctx_1024', 'mask_BxS2_bf1', 'L0_xattn_Wq', 'L0_xattn_Wk', 'L0_xattn_Wv', 'L0_xattn_Wo', 'L0_xattn_bo',
        'L0_ffn_gate_w', 'L0_ffn_w_gate', 'L0_ffn_w_up', 'L0_ffn_w_down', 'L0_ffn_ws_gate', 'L0_ffn_ws_up',
        'L0_ffn_ws_down']


def kernel(**inputs):
    import numpy as _np
    import concourse.bacc as _bacc
    from concourse import mybir as _mybir
    from concourse.bass_utils import run_bass_kernel_spmd as _run

    nc = _bacc.Bacc("TRN2", target_bir_lowering=False, num_devices=1)
    arrays, args = {}, []
    for name in _INS:
        a = _np.ascontiguousarray(inputs[name])
        if a.dtype == _np.bool_:
            a = a.view(_np.uint8)
        arrays[f"in_{name}"] = a
        args.append(nc.dram_tensor(f"in_{name}", a.shape, _mybir.dt.from_np(a.dtype), kind="ExternalInput").ap())
    shape = inputs['x'].shape
    args.append(nc.dram_tensor("out_x", tuple(shape), _mybir.dt.float32, kind="ExternalOutput").ap())
    xattn_moe_kernel(nc, *args)
    r = _run(nc, [arrays], core_ids=[0])
    return r.results[0]["out_x"]
```

```python
from contextlib import ExitStack

import concourse.bass as bass
from concourse import mybir

F32 = mybir.dt.float32
F32R = mybir.dt.float32r
BF16 = mybir.dt.bfloat16
ALU = mybir.AluOpType
ACT = mybir.ActivationFunctionType
AX_X = mybir.AxisListType.X

P = 128
HEADS = 16
HD = 64
SEQ = 64
EXPERTS = 16
MID = 64
TOP_SCALE = 2.5
LN_EPS = 1e-5
SATURATED = 20.0
MASKED = -1e30


def at_least(eng, sem, value):
    if isinstance(value, int) and value <= 0:
        return
    eng.wait_ge(sem, value)


def xattn_moe_kernel(nc, x, ctx_in, mask, Wq, Wk, Wv, Wo, bo, gate_w, w_gate, w_up, w_down,
                     ws_gate, ws_up, ws_down, out):
    batches = x.shape[0]
    PAIRS = batches // 2
    BODIES = PAIRS // 4
    GROUPS = PAIRS // 2
    GT = 2 * P
    BLOCKS = EXPERTS // 2 + 1
    QUADS = PAIRS // 4
    LAG = 3
    QT = 4 * P

    x_tiles = x.rearrange("(t b) s d -> (t b s) d", b=2).rearrange("(t p) d -> p t d", p=P)
    out_tiles = out.rearrange("(t b) s d -> (t b s) d", b=2).rearrange("(t p) d -> p t d", p=P)

    with ExitStack() as stack:
        def sb(name, shape, dt=F32):
            return stack.enter_context(nc.sbuf_tensor(name, shape, dt))

        def sem(name):
            return stack.enter_context(nc.semaphore(name))

        bank = [stack.enter_context(nc.psum_tensor(f"bank{i}", [P, 512], F32)) for i in range(8)]
        rot = bank[0:3]
        score_bank = bank[3:5]
        pv_bank = bank[5:7]
        acc = bank[7]

        xall = sb("xall", [P, PAIRS, P])
        keys = sb("keys", [P, 2, HEADS, GT])
        r_hi = sb("r_hi", [P, 2, HEADS, GT], F32R)
        r_lo = sb("r_lo", [P, 2, HEADS, GT], F32R)
        pt_hi = sb("pt_hi", [P, 8, P], F32R)
        pt_lo = sb("pt_lo", [P, 8, P], F32R)
        probs = sb("probs", [P, HEADS, SEQ])
        craw = sb("craw", [P, 2, 4, P])
        c_hi = sb("c_hi", [P, 2, 4, P], F32R)
        c_lo = sb("c_lo", [P, 2, 4, P], F32R)
        ct_hi = sb("ct_hi", [P, GT], F32R)
        ct_lo = sb("ct_lo", [P, GT], F32R)
        xt = sb("xt", [P, 2, GT])
        xn = sb("xn", [P, 2, P])
        attn_t = sb("attn_t", [P, GT])
        m_hi = sb("m_hi", [P, HEADS, P], F32R)
        m_lo = sb("m_lo", [P, HEADS, P], F32R)
        b_hi = sb("b_hi", [P, HEADS, P], F32R)
        b_lo = sb("b_lo", [P, HEADS, P], F32R)
        wg_hi = sb("wg_hi", [P, BLOCKS, P], F32R)
        wg_lo = sb("wg_lo", [P, BLOCKS, P], F32R)
        wu_hi = sb("wu_hi", [P, BLOCKS - 1, P], F32R)
        wu_lo = sb("wu_lo", [P, BLOCKS - 1, P], F32R)
        maskb = sb("maskb", [P, PAIRS, SEQ], BF16)
        tri = sb("tri", [P, SEQ])
        ident = sb("ident", [P, P])
        ident_b = sb("ident_b", [P, P], BF16)
        mask_u8 = sb("mask_u8", [2, PAIRS, SEQ], mask.dtype)
        half_of = sb("half_of", [2, P], BF16)
        bo_col = sb("bo_col", [P, 1])
        gw_row = sb("gw_row", [EXPERTS, P])
        gw_t = sb("gw_t", [P, EXPERTS])
        wait_cell = sb("wait_cell", [P, 1])
        zero_col = sb("zero_col", [P, 1])
        stats = sb("stats", [P, 2, 6])
        mean_var = sb("mean_var", [P, 2, 2])
        var_eps = sb("var_eps", [P, 2, 1])
        rstd = sb("rstd", [P, 2, 1])
        stats2 = sb("stats2", [P, 2, 6])
        mean_var2 = sb("mean_var2", [P, 2, 2])
        mean2 = sb("mean2", [P, PAIRS, 1])
        var_eps2 = sb("var_eps2", [P, PAIRS, 1])
        rstd2 = sb("rstd2", [P, PAIRS, 1])
        minus_half = sb("minus_half", [P, 1, 1])
        row_max = sb("row_max", [P, HEADS])
        row_sum = sb("row_sum", [P, HEADS])
        nan_probe = sb("nan_probe", [P, HEADS])
        inv_raw = sb("inv_raw", [P, HEADS])
        inv = sb("inv", [P, HEADS])
        score = sb("score", [P, 4, EXPERTS + 8])
        best = sb("best", [P, 4, 8])
        taken = sb("taken", [P, 4, 8])
        marked = sb("marked", [P, 4, EXPERTS + 8])
        best_sum = sb("best_sum", [P, 4, 1])
        best_inv = sb("best_inv", [P, 4, 1])
        picked = sb("picked", [P, 4, EXPERTS])
        route = sb("route", [P, 4, EXPERTS])
        route2 = sb("route2", [P, 4, 2 * EXPERTS], F32R)

        keys_flat = keys[:].rearrange("p a h t -> p (a h t)")
        wq_s = keys_flat[0:HD, 0:2048].rearrange("p (h e) -> p h e", h=HEADS)
        wk_s = keys_flat[0:HD, 2048:4096].rearrange("p (h e) -> p h e", h=HEADS)
        wv_s = keys_flat[0:HD, 4096:6144].rearrange("p (h e) -> p h e", h=HEADS)
        wo_t = keys_flat[0:HD, 6144:8192].rearrange("p (h e) -> p h e", h=HEADS)
        mask_neg = keys_flat[0:2, 0:1024].bitcast(BF16).rearrange("b (t k) -> b t k", k=SEQ)
        craw_flat = craw[:].rearrange("p a b e -> p (a b e)")
        sel_f = craw_flat[0:2 * EXPERTS, :].rearrange("p (n r) -> p n r", n=8)
        sel = pt_lo[0:2 * EXPERTS]
        route_t = pt_hi[0:2 * EXPERTS, 0:4, :].rearrange("p n t -> p (n t)")
        wo_s = probs[:].rearrange("p h k -> p (h k)")
        wg_raw = keys_flat[:, 0:1152]
        wu_raw = keys_flat[:, 1152:2176]
        wd_raw = keys_flat[:, 2176:3328]
        sg = keys_flat[:, 4096:5632].rearrange("p (n t) -> p n t", n=3)
        hid = keys_flat[:, 5632:8192].rearrange("p (n t) -> p n t", n=5)
        place = lambda n: n % 4 if n < BLOCKS - 1 else 4
        y_t = craw_flat[:, 0:QT]
        out_sb = craw_flat[:, QT:2 * QT].rearrange("p (n d) -> p n d", n=4)
        logit_fix, logit, logit_inv, logit_silu = [
            xn[:].rearrange("p k e -> p (k e)")[:, 64 * k:64 * k + 64].rearrange("p (t e) -> p t e", e=EXPERTS)
            for k in range(4)]
        wd_hi = m_hi[:, 0:BLOCKS, :]
        wd_lo = m_lo[:, 0:BLOCKS, :]
        rh_flat = r_hi[:].rearrange("p a h t -> p (a h t)")
        rl_flat = r_lo[:].rearrange("p a h t -> p (a h t)")
        x2_hi = rh_flat[:, 0:4096].rearrange("p (g t) -> p g t", g=QUADS)
        x2_lo = rl_flat[:, 0:4096].rearrange("p (g t) -> p g t", g=QUADS)
        hid_hi = rh_flat[:, 4096:6656].rearrange("p (n t) -> p n t", n=5)
        hid_lo = rl_flat[:, 4096:6656].rearrange("p (n t) -> p n t", n=5)
        probs_flat = probs[:].rearrange("p h k -> p (h k)")
        x2_f = probs_flat[:, 0:QT]
        xn2 = probs_flat[:, QT:2 * QT].rearrange("p (n d) -> p n d", n=4)

        flat3 = lambda ap: ap.rearrange("p n d -> p (n d)")
        ffn_parts = [(flat3(wg_hi[:]), flat3(wg_lo[:]), wg_raw), (flat3(wu_hi[:]), flat3(wu_lo[:]), wu_raw),
                     (flat3(wd_hi[:, 0:8, :]), flat3(wd_lo[:, 0:8, :]), wd_raw[:, 0:1024]),
                     (wd_hi[0:MID, 8, :], wd_lo[0:MID, 8, :], wd_raw[0:MID, 1024:1152])]

        wk_in, wo_in, x_first_in, x_rest_in = sem("wk_in"), sem("wo_in"), sem("x_first_in"), sem("x_rest_in")
        wv_in, mask_in, small_in, ffn_in = sem("wv_in"), sem("mask_in"), sem("small_in"), sem("ffn_in")
        ctx_landed = [sem("ctx_even_in"), sem("ctx_odd_in")]
        pool_step, consts_made = sem("pool_step"), sem("consts_made")
        sel_made, mask_neg_made = sem("sel_made"), sem("mask_neg_made")
        m_done, m_hi_made, m_lo_made = sem("m_done"), sem("m_hi_made"), sem("m_lo_made")
        wot_done, wot_copied = sem("wot_done"), sem("wot_copied")
        b_done, b_hi_made, b_lo_made = sem("b_done"), sem("b_hi_made"), sem("b_lo_made")
        mask_spread, mask_made = sem("mask_spread"), sem("mask_made")
        ctx_hi_made, ctx_lo_made = sem("ctx_hi_made"), sem("ctx_lo_made")
        ct_done, ct_hi_made, ct_lo_made = sem("ct_done"), sem("ct_hi_made"), sem("ct_lo_made")
        keys_done, keys_copied = sem("keys_done"), sem("keys_copied")
        ln_step, var_made, rstd_made = sem("ln_step"), sem("var_made"), sem("rstd_made")
        xn_made, xt_done, xt_copied = sem("xn_made"), sem("xt_done"), sem("xt_copied")
        scores_done, max_made, shifted, exp_made = sem("scores_done"), sem("max_made"), sem("shifted"), sem("exp_made")
        sum_made, inv_step, inv_made, probs_made = sem("sum_made"), sem("inv_step"), sem("inv_made"), sem("probs_made")
        pt_done, pt_hi_made, pt_lo_made = sem("pt_done"), sem("pt_hi_made"), sem("pt_lo_made")
        pv_done, r_hi_made, r_lo_made = sem("pv_done"), sem("r_hi_made"), sem("r_lo_made")
        attn_done, attn_copied, attn_turned, x2_made = sem("attn_done"), sem("attn_copied"), sem("attn_turned"), sem("x2_made")
        ffn_hi_made, ffn_lo_made = sem("ffn_hi_made"), sem("ffn_lo_made")
        gwt_done, gwt_copied = sem("gwt_done"), sem("gwt_copied")
        sel_f_made = sem("sel_f_made")
        ln2_step, var2_made, rstd2_made = sem("ln2_step"), sem("var2_made"), sem("rstd2_made")
        xn2_made, x2t_done = sem("xn2_made"), sem("x2t_done")
        x2_hi_made, x2_f_made, x2_lo_made = sem("x2_hi_made"), sem("x2_f_made"), sem("x2_lo_made")
        logit_done, logit_step, logit_made, silu_of_logit = sem("logit_done"), sem("logit_step"), sem("logit_made"), sem("silu_of_logit")
        top_step, route_made, route_turned, route_copied = sem("top_step"), sem("route_made"), sem("route_turned"), sem("route_copied")
        fill_made, route_step = sem("fill_made"), sem("route_step")
        gate_done, up_done, silu_made, hid_made = sem("gate_done"), sem("up_done"), sem("silu_made"), sem("hid_made")
        prod_made, hid_hi_made, hid_lo_made = sem("prod_made"), sem("hid_hi_made"), sem("hid_lo_made")
        y_done, y_copied, y_turned, out_made, out_stored = sem("y_done"), sem("y_copied"), sem("y_turned"), sem("out_made"), sem("out_stored")

        block = stack.enter_context(nc.Block())

        def once(bank_):
            return bank_[:].rearrange("p (b a k) -> p b a k", a=2, k=SEQ)[:, :, 0, :]

        @block.sync
        def _(sp):
            def load_ctx(group, parity):
                for half in range(2):
                    sp.dma_start(craw[half * SEQ:(half + 1) * SEQ, parity],
                                 ctx_in[bass.ds(4 * group, 4)].rearrange("b k e -> k b e")
                                 ).then_inc(ctx_landed[parity], 16)

            sp.dma_start(wq_s, Wq.rearrange("(h d) e -> d h e", d=HD)).then_inc(wk_in, 16)
            sp.dma_start(wk_s, Wk.rearrange("(h d) e -> d h e", d=HD)).then_inc(wk_in, 16)
            sp.dma_start(wo_s, Wo).then_inc(wo_in, 16)
            sp.dma_start(wv_s, Wv.rearrange("(h d) e -> d h e", d=HD)).then_inc(wv_in, 16)
            load_ctx(0, 0)
            sp.dma_start(xall[:, 0:4, :], x_tiles[:, 0:4, :]).then_inc(x_first_in, 16)
            load_ctx(1, 1)
            sp.dma_start(mask_u8[:], mask.rearrange("(t b) k -> b t k", b=2)).then_inc(mask_in, 16)
            sp.dma_start(bo_col[:], bo.rearrange("(d a) -> d a", a=1)).then_inc(small_in, 16)
            sp.dma_start(gw_row[:], gate_w).then_inc(small_in, 16)
            sp.dma_start(xall[:, 4:PAIRS, :], x_tiles[:, 4:PAIRS, :]).then_inc(x_rest_in, 16)

            def body(i, last):
                for parity in range(2):
                    if last:
                        continue
                    group = 2 * i + parity
                    sp.wait_ge(ctx_lo_made, group + 1)
                    sp.wait_ge(ct_done, group + 1)
                    load_ctx(group + 2, parity)

            with sp.Fori(0, BODIES - 1) as i:
                body(i, False)

            sp.wait_ge(scores_done, 2 * (PAIRS - 2))
            sp.dma_start(wg_raw[:, 0:1024].rearrange("p (e m) -> p e m", m=MID),
                         w_gate.rearrange("e h m -> h e m")).then_inc(ffn_in, 16)
            sp.dma_start(wg_raw[:, 1024:1088], ws_gate).then_inc(ffn_in, 16)
            sp.dma_start(wg_raw[:, 1088:1152], ws_up).then_inc(ffn_in, 16)
            sp.dma_start(wu_raw.rearrange("p (e m) -> p e m", m=MID),
                         w_up.rearrange("e h m -> h e m")).then_inc(ffn_in, 16)
            sp.dma_start(wd_raw[:, 0:1024].rearrange("p (n d) -> p n d", d=P),
                         w_down.rearrange("(n a) m d -> (a m) n d", a=2)).then_inc(ffn_in, 16)
            sp.dma_start(wd_raw[0:MID, 1024:1152], ws_down).then_inc(ffn_in, 16)

            with sp.Fori(0, QUADS) as quad:
                sp.wait_ge(out_made, quad + 1)
                sp.dma_start(out_tiles[:, bass.ds(4 * quad, 4), :], out_sb).then_inc(out_stored, 16)
            sp.wait_ge(out_stored, 16 * QUADS)

        @block.gpsimd
        def _(pool):
            steps = [0]

            def step(ins):
                steps[0] += 1
                ins.then_inc(pool_step, 1)
                pool.wait_ge(pool_step, steps[0])

            step(nc.gpsimd.memset(ident[:], 0.0))
            step(nc.gpsimd.affine_select(out=ident[:], in_=ident[:], compare_op=ALU.not_equal, fill=1.0,
                                         base=0, pattern=[[-1, P]], channel_multiplier=1))
            nc.gpsimd.tensor_copy(ident_b[:], ident[:]).then_inc(consts_made, 1)
            step(nc.gpsimd.memset(tri[:], 0.0))
            for half in range(2):
                rows = tri[half * SEQ:(half + 1) * SEQ, :]
                nc.gpsimd.affine_select(out=rows, in_=rows, compare_op=ALU.is_ge, fill=MASKED, base=0,
                                        pattern=[[-1, SEQ]], channel_multiplier=1).then_inc(consts_made, 1)
            step(nc.gpsimd.memset(half_of[:], 1.0))
            step(nc.gpsimd.affine_select(out=half_of[:], in_=half_of[:], compare_op=ALU.is_ge, fill=0.0,
                                         base=0, pattern=[[1, P]], channel_multiplier=-SEQ))
            nc.gpsimd.affine_select(out=half_of[:], in_=half_of[:], compare_op=ALU.is_ge, fill=0.0,
                                    base=SEQ - 1, pattern=[[-1, P]], channel_multiplier=SEQ).then_inc(consts_made, 1)

            def split_ctx(group, parity, round_):
                at_least(pool, pv_done, 8 * (group - 1))
                pool.wait_ge(ctx_landed[parity], 32 * (round_ + 1))
                nc.gpsimd.tensor_tensor(c_hi[:, parity], craw[:, parity],
                                        zero_col[:].unsqueeze(1).to_broadcast([P, 4, P]), ALU.add
                                        ).then_inc(ctx_hi_made, 1)
                pool.wait_ge(ctx_hi_made, group + 1)
                nc.gpsimd.tensor_tensor(c_lo[:, parity], craw[:, parity], c_hi[:, parity],
                                        ALU.subtract).then_inc(ctx_lo_made, 1)

            def normalise(pair):
                pool.wait_ge(inv_made, pair + 1)
                for half in range(2):
                    heads = slice(8 * half, 8 * half + 8)
                    nc.gpsimd.tensor_tensor(probs[:, heads, :], probs[:, heads, :],
                                            inv[:, heads].unsqueeze(2).to_broadcast([P, 8, SEQ]),
                                            ALU.mult).then_inc(probs_made, 1)

            nc.gpsimd.memset(minus_half[:], -0.5).then_inc(fill_made, 1)
            nc.gpsimd.memset(zero_col[:], 0.0).then_inc(fill_made, 1)
            pool.wait_ge(fill_made, 2)

            def deviation(group):
                pool.wait_ge(var_made, group + 1)
                nc.gpsimd.tensor_tensor(rstd[:], var_eps[:], minus_half[:].to_broadcast([P, 2, 1]), ALU.pow
                                        ).then_inc(rstd_made, 1)

            def deviation2(groups):
                pool.wait_ge(var2_made, groups.stop)
                tiles = slice(2 * groups.start, 2 * groups.stop)
                nc.gpsimd.tensor_tensor(rstd2[:, tiles, :], var_eps2[:, tiles, :],
                                        minus_half[:].to_broadcast([P, 2 * len(groups), 1]), ALU.pow
                                        ).then_inc(rstd2_made, 1)

            deviation(0)
            split_ctx(0, 0, 0)
            deviation(1)
            split_ctx(1, 1, 0)
            nc.gpsimd.memset(score[:], -1.0).then_inc(fill_made, 1)
            nc.gpsimd.memset(taken[:], -1.0).then_inc(fill_made, 1)
            normalise(0)

            def body(i, last):
                for s in range(4):
                    pair, parity = 4 * i + s, s // 2
                    if s % 2 == 1 and not last:
                        deviation(2 * i + parity + 2)
                    if last and s == 1:
                        deviation2(range(0, GROUPS - 4))
                    if not (last and s == 3):
                        normalise(pair + 1)
                    if s % 2 == 1 and not last:
                        split_ctx(2 * i + parity + 2, parity, i + 1)
                    if last and s == 0:
                        spread_ones()

            def spread_ones():
                pool.wait_ge(ctx_lo_made, GROUPS)
                pool.wait_ge(ct_done, GROUPS)
                step(nc.gpsimd.memset(sel_f, 0.0))
                for first_row in (0, EXPERTS):
                    ins = nc.gpsimd.affine_select(out=sel_f, in_=sel_f, compare_op=ALU.not_equal, fill=1.0,
                                                  base=-first_row, pattern=[[-2, 8], [-1, 2], [0, MID]],
                                                  channel_multiplier=1)
                    if first_row == 0:
                        step(ins)
                    else:
                        ins.then_inc(sel_f_made, 1)

            with pool.Fori(0, BODIES - 1) as i:
                body(i, False)
            body(BODIES - 1, True)

            def weight_low(k):
                hi, lo, raw = ffn_parts[k]
                pool.wait_ge(ffn_hi_made, k + 1)
                nc.gpsimd.tensor_tensor(lo, raw, hi, ALU.subtract).then_inc(ffn_lo_made, 1)

            def x2_low(quad):
                pool.wait_ge(x2_f_made, quad + 1)
                nc.gpsimd.tensor_tensor(x2_lo[:, bass.ds(quad, 1), :].rearrange("p a t -> p (a t)"), x2_f,
                                        x2_hi[:, bass.ds(quad, 1), :].rearrange("p a t -> p (a t)"),
                                        ALU.subtract).then_inc(x2_lo_made, 1)

            def hid_low(quad, n):
                rows = P if n < BLOCKS - 1 else MID
                step_no = BLOCKS * quad + n
                pool.wait_ge(hid_hi_made, step_no + 1)
                at = place(n)
                nc.gpsimd.tensor_tensor(hid_lo[0:rows, at], hid[0:rows, at], hid_hi[0:rows, at],
                                        ALU.subtract).then_inc(hid_lo_made, 1)

            def quad_body(quad, first, last):
                for n in range(BLOCKS):
                    hid_low(quad, n)
                    if n == 1 and not last:
                        x2_low(quad + 1)
                    if n == 4 and first:
                        deviation2(range(GROUPS - 4, GROUPS))

            weight_low(0)
            weight_low(1)
            x2_low(0)
            weight_low(2)
            weight_low(3)
            quad_body(0, True, False)
            with pool.Fori(1, QUADS - 1) as quad:
                quad_body(quad, False, False)
            quad_body(QUADS - 1, False, True)

        @block.tensor
        def _(pe):
            def three(out_, a_hi, a_lo, b_hi_, b_lo_, start=True, stop=True):
                nc.tensor.matmul(out_, a_hi, b_hi_, start=start, stop=False)
                nc.tensor.matmul(out_, a_lo, b_hi_, start=False, stop=False)
                return nc.tensor.matmul(out_, a_hi, b_lo_, start=False, stop=stop)

            pe.wait_ge(wk_in, 32)
            for c in range(4):
                for j in range(4):
                    h = 4 * c + j
                    last = nc.tensor.matmul(bank[c][:, j * P:(j + 1) * P], wk_s[:, h, :], wq_s[:, h, :],
                                            start=True, stop=True)
                last.then_inc(m_done, 1)
            pe.wait_ge(wo_in, 16)
            pe.wait_ge(consts_made, 4)
            for c in range(4):
                for j in range(4):
                    h = 4 * c + j
                    last = nc.tensor.transpose(bank[4 + c][0:HD, j * P:(j + 1) * P],
                                               wo_s[:, h * HD:(h + 1) * HD], ident[:])
                last.then_inc(wot_done, 1)
            pe.wait_ge(wv_in, 16)
            for c in range(4):
                pe.wait_ge(m_lo_made, c + 1)
                pe.wait_ge(wot_copied, c + 1)
                for j in range(4):
                    h = 4 * c + j
                    last = nc.tensor.matmul(bank[c][:, j * P:(j + 1) * P], wv_s[:, h, :], wo_t[:, h, :],
                                            start=True, stop=True)
                last.then_inc(b_done, 1)
            pe.wait_ge(mask_neg_made, 1)
            for c in range(4):
                nc.tensor.matmul(bank[4 + c][:], half_of[:],
                                 mask_neg.rearrange("b t k -> b (t k)")[:, 512 * c:512 * c + 512],
                                 start=True, stop=True).then_inc(mask_spread, 1)
            pe.wait_ge(b_lo_made, 4)
            pe.wait_ge(mask_made, 4)

            def turn_ctx(group, parity, round_):
                pe.wait_ge(ctx_landed[parity], 32 * (round_ + 1))
                for b in range(4):
                    last = nc.tensor.transpose(rot[1][:, b * P:(b + 1) * P], craw[:, parity, b, :], ident[:])
                last.then_inc(ct_done, 1)

            def turn_x(group, into):
                pe.wait_ge(xn_made, group + 1)
                for k in range(2):
                    last = nc.tensor.transpose(into[:, k * P:(k + 1) * P], xn[:, k, :], ident[:])
                last.then_inc(xt_done, 1)

            def project_keys(j, into):
                for a in range(2):
                    h = 2 * j + a
                    last = three(into[:, a * GT:(a + 1) * GT], m_hi[:, h, :], m_lo[:, h, :], ct_hi[:], ct_lo[:])
                last.then_inc(keys_done, 1)

            def scores(pair, s):
                parity, r = s // 2, s % 2
                group = (pair - r) // 2 if isinstance(pair, int) else None
                for half in range(2):
                    at_least(pe, shifted, 2 * (pair - 1) + half + 1)
                    seen = maskb[:, bass.ds(pair, 1), :].to_broadcast([P, 8, SEQ])
                    nc.tensor.matmul(score_bank[half][:], ident_b[:], seen, start=True, stop=False,
                                     skip_group_check=True)
                    for b in range(2):
                        col = r * P + b * SEQ
                        last = nc.tensor.matmul(score_bank[half][b * SEQ:(b + 1) * SEQ, :],
                                                xt[:, parity, col:col + SEQ],
                                                keys[:, parity, 8 * half:8 * half + 8, col:col + SEQ],
                                                start=False, stop=True, skip_group_check=True)
                    last.then_inc(scores_done, 1)

            def turn_probs(pair, v, into):
                pe.wait_ge(probs_made, 2 * pair + v + 1)
                for k in range(4):
                    src = probs[:, 8 * v + 2 * k:8 * v + 2 * k + 2, :].rearrange("p h k -> p (h k)")
                    last = nc.tensor.transpose(into[:, k * P:(k + 1) * P], src, ident[:])
                last.then_inc(pt_done, 1)

            def probs_by_ctx(pair, s, b):
                parity, r = s // 2, s % 2
                for part in range(3):
                    w = c_lo if part == 1 else c_hi
                    m = pt_lo if part == 2 else pt_hi
                    for h2 in range(2):
                        if part == 0:
                            at_least(pe, r_lo_made, 4 * pair + 2 * b + h2 - 1)
                        rows = slice(h2 * SEQ, (h2 + 1) * SEQ)
                        last = nc.tensor.matmul(pv_bank[h2][:], w[rows, parity, 2 * r + b, :],
                                                m[rows, :, b * SEQ:(b + 1) * SEQ],
                                                start=(part == 0), stop=(part == 2))
                        if part == 2:
                            last.then_inc(pv_done, 1)

            def add_heads(group, parity, heads):
                for h in heads:
                    last = three(acc[:, 0:GT], b_hi[:, h, :], b_lo[:, h, :], r_hi[:, parity, h, :],
                                 r_lo[:, parity, h, :], start=(h == 0), stop=(h == HEADS - 1))
                if heads[-1] == HEADS - 1:
                    last.then_inc(attn_done, 1)

            def turn_attn(group, into):
                pe.wait_ge(attn_copied, group + 1)
                for k in range(2):
                    last = nc.tensor.transpose(into[:, k * P:(k + 1) * P], attn_t[:, k * P:(k + 1) * P], ident[:])
                last.then_inc(attn_turned, 1)

            gate_bank, up_bank, spread_bank, misc = bank[0:2], bank[2:4], bank[4:6], bank[6]

            def turn_x2(quad, into):
                pe.wait_ge(xn2_made, quad + 1)
                for k in range(4):
                    last = nc.tensor.transpose(into[:, k * P:(k + 1) * P], xn2[:, k, :], ident[:])
                last.then_inc(x2t_done, 1)

            def logits(quad, into):
                pe.wait_ge(x2_f_made, quad + 1)
                for k in range(4):
                    last = nc.tensor.matmul(into[:, k * EXPERTS:(k + 1) * EXPERTS], x2_f[:, k * P:(k + 1) * P],
                                            gw_t[:], start=True, stop=True)
                last.then_inc(logit_done, 1)

            def turn_route(quad, into):
                pe.wait_ge(route_made, quad + 1)
                at_least(pe, out_made, quad - 1)
                for k in range(4):
                    last = nc.tensor.transpose(into[0:2 * EXPERTS, k * P:(k + 1) * P],
                                               route2[:, k, :].bitcast(F32), ident[:])
                last.then_inc(route_turned, 1)

            pe.wait_ge(small_in, 32)
            nc.tensor.transpose(misc[:, 0:EXPERTS], gw_row[:], ident[0:EXPERTS, 0:EXPERTS]).then_inc(gwt_done, 1)

            turn_ctx(0, 0, 0)
            turn_x(0, rot[0])
            pe.wait_ge(ct_lo_made, 1)
            for j in range(8):
                if j == 1:
                    pe.wait_ge(xt_copied, 1)
                if j == 2:
                    pe.wait_ge(ct_lo_made, 1)
                at_least(pe, keys_copied, j - 2)
                project_keys(j, rot[(j + 2) % 3])
            pe.wait_ge(keys_copied, 6)
            turn_ctx(1, 1, 0)
            pe.wait_ge(ct_lo_made, 2)
            project_keys(0, rot[1])
            pe.wait_ge(keys_copied, 7)
            project_keys(1, rot[2])
            pe.wait_ge(keys_copied, 8)
            project_keys(2, rot[0])
            scores(0, 0)
            pe.wait_ge(keys_copied, 9)
            project_keys(3, rot[1])

            def body(i, first, last):
                for s in range(4):
                    pair, parity, r = 4 * i + s, s // 2, s % 2
                    group = 2 * i + parity
                    last_group = last and parity == 1
                    if not (last and s == 3):
                        if r == 0:
                            at_least(pe, keys_copied, 8 * group + 8)
                        else:
                            pe.wait_ge(xt_copied, group + 2)
                            pe.wait_ge(keys_copied, 8 * (group + 1) + 8)
                        scores(pair + 1, (s + 1) % 4)
                    at_least(pe, pt_lo_made, 2 * pair)
                    if r == 0:
                        if not last_group:
                            pe.wait_ge(keys_copied, 8 * (group + 1) + 3)
                        turn_probs(pair, 0, rot[0])
                        if not last_group:
                            pe.wait_ge(keys_copied, 8 * (group + 1) + 4)
                        turn_probs(pair, 1, rot[1])
                    else:
                        if not last_group:
                            pe.wait_ge(keys_copied, 8 * (group + 1) + 8)
                        else:
                            at_least(pe, x2_made, group - 2)
                        turn_probs(pair, 0, rot[2])
                        if not last_group:
                            pe.wait_ge(xt_copied, group + 2)
                        turn_probs(pair, 1, rot[0])
                    after_first = not (first and parity == 0)
                    if after_first:
                        if r == 0:
                            pe.wait_ge(r_lo_made, 8 * group)
                            at_least(pe, attn_copied, group - 1)
                        add_heads(group - 1, 1 - parity, range(8 * r, 8 * r + 4))
                    if r == 0 and not last_group:
                        project_keys(4, rot[2])
                        pe.wait_ge(pt_lo_made, 2 * pair + 1)
                        project_keys(5, rot[0])
                    if r == 1 and not last:
                        pe.wait_ge(ct_lo_made, group + 3)
                        project_keys(0, rot[1])
                        pe.wait_ge(pt_lo_made, 2 * pair + 1)
                        project_keys(1, rot[2])
                    pe.wait_ge(pt_lo_made, 2 * pair + 2)
                    if r == 0:
                        pe.wait_ge(ctx_lo_made, group + 1)
                    probs_by_ctx(pair, s, 0)
                    if last and s == 3:
                        turn_x2(0, rot[1])
                    if r == 0 and not last_group:
                        project_keys(6, rot[1])
                        pe.wait_ge(keys_copied, 8 * (group + 1) + 5)
                        project_keys(7, rot[2])
                        pe.wait_ge(keys_copied, 8 * (group + 1) + 6)
                        turn_x(group + 1, rot[0])
                        if not last:
                            pe.wait_ge(keys_copied, 8 * (group + 1) + 7)
                            turn_ctx(group + 2, parity, i + 1)
                    if r == 1 and not last:
                        project_keys(2, rot[0])
                        pe.wait_ge(keys_copied, 8 * (group + 2) + 1)
                        project_keys(3, rot[1])
                    if r == 1 and not first:
                        pe.wait_ge(keys_copied, 8 * (group + 2) + 2) if not last else pe.wait_ge(pt_lo_made, 2 * pair + 1)
                        turn_attn(group - 2, rot[2])
                    if after_first:
                        add_heads(group - 1, 1 - parity, range(8 * r + 4, 8 * r + 8))
                    if last and s == 3:
                        pe.wait_ge(shifted, 2 * PAIRS)
                        logits(0, score_bank[0])
                    if first and s == 0:
                        pe.wait_ge(gwt_copied, 1)
                    probs_by_ctx(pair, s, 1)

            body(0, True, False)
            with pe.Fori(1, BODIES - 1) as i:
                body(i, False, False)
            body(BODIES - 1, False, True)
            pe.wait_ge(x2_f_made, 1)
            turn_attn(GROUPS - 2, rot[1])

            def rest_of_attention():
                pe.wait_ge(r_lo_made, 4 * PAIRS)
                pe.wait_ge(attn_copied, GROUPS - 1)
                add_heads(GROUPS - 1, 1, range(HEADS))

            def up(quad, n):
                hi = x2_hi[:, bass.ds(quad, 1), :].rearrange("p a t -> p (a t)")
                lo = x2_lo[:, bass.ds(quad, 1), :].rearrange("p a t -> p (a t)")
                q = n % 2
                step_no = BLOCKS * quad + n
                if n < BLOCKS - 1:
                    at_least(pe, prod_made, step_no - 1 if n > 1 else step_no - 2)
                if isinstance(quad, int) and quad == 0 and n == 1:
                    pe.wait_ge(x2_made, GROUPS - 1)
                if n == BLOCKS - 1:
                    at_least(pe, hid_made, 8 * quad + n - 1)
                    three(spread_bank[q][:], wg_hi[:, n, :], wg_lo[:, n, :], hi, lo).then_inc(gate_done, 1)
                    return
                three(gate_bank[q][:], wg_hi[:, n, :], wg_lo[:, n, :], hi, lo).then_inc(gate_done, 1)
                if isinstance(quad, int) and quad == 0 and n < 2:
                    pe.wait_ge(x2_made, GROUPS - 2) if n == 0 else pe.wait_ge(logit_made, 1)
                at_least(pe, hid_made, 8 * quad + n - 1)
                three(up_bank[q][:], wu_hi[:, n, :], wu_lo[:, n, :], hi, lo)

            def spread(quad, n):
                q = n % 2
                if n == 0:
                    pe.wait_ge(route_copied, quad + 1)
                    pe.wait_ge(sel_made, 1)
                    at_least(pe, prod_made, BLOCKS * quad)
                nc.tensor.matmul(spread_bank[q][:], sel[:, n, :], route_t, start=True, stop=True
                                 ).then_inc(up_done, 1)

            def down(quad, n):
                rows = P if n < BLOCKS - 1 else MID
                if n == 0:
                    at_least(pe, y_copied, quad)
                    if isinstance(quad, int) and quad == 0:
                        pe.wait_ge(x2_made, GROUPS)
                        pe.wait_ge(ffn_lo_made, 4)
                pe.wait_ge(hid_lo_made, BLOCKS * quad + n + 1)
                last = three(acc[:], wd_hi[0:rows, n, :], wd_lo[0:rows, n, :], hid_hi[0:rows, place(n)],
                             hid_lo[0:rows, place(n)], start=(n == 0), stop=(n == BLOCKS - 1))
                if n == BLOCKS - 1:
                    last.then_inc(y_done, 1)

            def quad_body(quad, first, last):
                for n in range(BLOCKS):
                    if n == 0:
                        pe.wait_ge(x2_lo_made, quad + 1)
                    if first and n == 1:
                        spread(quad, n)
                        continue_first(quad)
                        continue
                    up(quad, n)
                    if first and n == 0:
                        rest_of_attention()
                        up(quad, 1)
                        turn_route(0, score_bank[1])
                    elif n == 0:
                        turn_route(quad, misc)
                    elif n < BLOCKS - 1:
                        spread(quad, n)
                    if n >= LAG:
                        down(quad, n - LAG)
                    elif not first:
                        down(quad - 1, BLOCKS - LAG + n)
                    if n == 0:
                        spread(quad, n)
                    if n == 1 and not last:
                        turn_x2(quad + 1, misc)
                    if n == 2 and not last:
                        logits(quad + 1, misc)
                    if n == 5 and not first:
                        turn_y(quad - 1, last)

            def continue_first(quad):
                pe.wait_ge(r_lo_made, 4 * PAIRS)
                turn_x2(quad + 1, misc)
                turn_attn(GROUPS - 1, acc[:, GT:2 * GT])

            def turn_y(quad, last):
                pe.wait_ge(y_copied, quad + 1)
                if not last:
                    pe.wait_ge(logit_made, quad + 3)
                for k in range(4):
                    ins = nc.tensor.transpose(misc[:, k * P:(k + 1) * P], y_t[:, k * P:(k + 1) * P], ident[:])
                ins.then_inc(y_turned, 1)

            pe.wait_ge(ffn_lo_made, 2)
            pe.wait_ge(pt_lo_made, 2 * PAIRS)
            quad_body(0, True, False)
            with pe.Fori(1, QUADS - 1) as quad:
                quad_body(quad, False, False)
            quad_body(QUADS - 1, False, True)
            for n in range(BLOCKS - LAG, BLOCKS):
                down(QUADS - 1, n)
            pe.wait_ge(out_made, QUADS - 1)
            turn_y(QUADS - 1, True)

        @block.scalar
        def _(act):
            copy = lambda dst, src: nc.scalar.activation(dst, src, ACT.Copy)

            for c in range(4):
                act.wait_ge(m_done, c + 1)
                copy(m_hi[:, 4 * c:4 * c + 4, :].rearrange("p h e -> p (h e)"), bank[c][:]).then_inc(m_hi_made, 1)
            for c in range(4):
                act.wait_ge(wot_done, c + 1)
                copy(wo_t[:, 4 * c:4 * c + 4, :].rearrange("p h e -> p (h e)"),
                     bank[4 + c][0:HD, :]).then_inc(wot_copied, 1)
            for c in range(4):
                act.wait_ge(b_done, c + 1)
                copy(b_hi[:, 4 * c:4 * c + 4, :].rearrange("p h e -> p (h e)"), bank[c][:]).then_inc(b_hi_made, 1)

            def ctx_t_high(group):
                act.wait_ge(ct_done, group + 1)
                copy(ct_hi[:].rearrange("p (b k) -> p b k", k=SEQ), once(rot[1])).then_inc(ct_hi_made, 1)

            def x_t(group, parity, src):
                act.wait_ge(xt_done, group + 1)
                at_least(act, scores_done, 4 * (group - 1))
                copy(xt[:, parity, :], src[:, 0:GT]).then_inc(xt_copied, 1)

            def keys_out(group, parity, j, src):
                act.wait_ge(keys_done, 8 * group + j + 1)
                if j == 0:
                    at_least(act, scores_done, 4 * (group - 1))
                copy(keys[:, parity, 2 * j:2 * j + 2, :].rearrange("p h t -> p (h t)"), src[:]
                     ).then_inc(keys_copied, 1)

            def exponentials(pair, half):
                act.wait_ge(shifted, 2 * pair + half + 1)
                part = probs[:, 8 * half:8 * half + 8, :]
                nc.scalar.activation(part, part, ACT.Exp, scale=HD ** -0.5).then_inc(exp_made, 1)

            def probs_t_high(pair, v, src):
                act.wait_ge(pt_done, 2 * pair + v + 1)
                if v == 0:
                    at_least(act, pv_done, 4 * pair)
                copy(pt_hi[:, 4 * v:4 * v + 4, :].rearrange("p h q -> p (h q)"), src[:]).then_inc(pt_hi_made, 1)

            def r_high(pair, s, b):
                parity, r = s // 2, s % 2
                for h2 in range(2):
                    act.wait_ge(pv_done, 4 * pair + 2 * b + h2 + 1)
                    col = r * P + b * SEQ
                    dst = r_hi[:, parity, :, col:col + SEQ].rearrange("p (n a) q -> p n a q", a=2)[:, :, h2, :]
                    copy(dst, pv_bank[h2][:].rearrange("p (n q) -> p n q", q=SEQ)).then_inc(r_hi_made, 1)

            def attn_out(group):
                act.wait_ge(attn_done, group + 1)
                at_least(act, attn_turned, group)
                nc.scalar.activation(attn_t[:], acc[:, 0:GT], ACT.Identity, bias=bo_col[:, 0:1]
                                     ).then_inc(attn_copied, 1)

            ctx_t_high(0)
            x_t(0, 0, rot[0])
            for j in range(8):
                keys_out(0, 0, j, rot[(j + 2) % 3])
            ctx_t_high(1)
            for j in range(4):
                keys_out(1, 1, j, rot[(j + 1) % 3])
            exponentials(0, 0)
            exponentials(0, 1)
            act.wait_ge(small_in, 32)

            misc = bank[6]
            act.wait_ge(gwt_done, 1)
            copy(gw_t[:], misc[:, 0:EXPERTS]).then_inc(gwt_copied, 1)

            def x2_high(quad, src):
                act.wait_ge(x2t_done, quad + 1)
                copy(x2_hi[:, bass.ds(quad, 1), :].rearrange("p a t -> p (a t)"), src[:]).then_inc(x2_hi_made, 1)
                copy(x2_f, src[:]).then_inc(x2_f_made, 1)

            def weight_high(k):
                hi, lo, raw = ffn_parts[k]
                act.wait_ge(ffn_in, 16 * 6)
                copy(hi, raw).then_inc(ffn_hi_made, 1)

            def body(i, first, last):
                for s in range(4):
                    pair, parity, r = 4 * i + s, s // 2, s % 2
                    group = 2 * i + parity
                    last_group = last and parity == 1
                    if r == 0 and not (first and parity == 0) and not (first and parity == 1):
                        attn_out(group - 2)
                    turned = (rot[0], rot[1]) if r == 0 else (rot[2], rot[0])
                    probs_t_high(pair, 0, turned[0])
                    probs_t_high(pair, 1, turned[1])
                    have_keys = not last_group if r == 0 else not last
                    key_args = ([(group + 1, 1 - parity, 4 + j, rot[(j + 2) % 3]) for j in range(4)] if r == 0 else
                                [(group + 2, parity, j, rot[(j + 1) % 3]) for j in range(4)])
                    for j in range(4):
                        if j == 2:
                            if last and s == 2:
                                weight_high(0)
                            if last and s == 3:
                                weight_high(1)
                            r_high(pair, s, 0)
                        if have_keys:
                            keys_out(*key_args[j])
                        if j < 2 and not (last and s == 3):
                            exponentials(pair + 1, j)
                    if r == 0 and not last_group:
                        x_t(group + 1, 1 - parity, rot[0])
                        if not last:
                            ctx_t_high(group + 2)
                    if last and s == 3:
                        x2_high(0, rot[1])
                        attn_out(GROUPS - 2)
                    r_high(pair, s, 1)

            body(0, True, False)
            with act.Fori(1, BODIES - 1) as i:
                body(i, False, False)
            body(BODIES - 1, False, True)

            gate_bank, spread_bank = bank[0:2], bank[4:6]

            def logit_silus(quad):
                act.wait_ge(logit_made, quad + 1)
                nc.scalar.activation(logit_silu[:], logit[:], ACT.Silu).then_inc(silu_of_logit, 1)

            def route_out(quad, src):
                act.wait_ge(route_turned, quad + 1)
                copy(route_t, src[0:2 * EXPERTS, :]).then_inc(route_copied, 1)

            def silu(quad, n):
                step_no = BLOCKS * quad + n
                rows = P if n < BLOCKS - 1 else MID
                act.wait_ge(gate_done, step_no + 1)
                at_least(act, prod_made, step_no - 2)
                src = gate_bank[n % 2] if n < BLOCKS - 1 else spread_bank[0]
                nc.scalar.activation(sg[0:rows, n % 3], src[0:rows, :], ACT.Silu
                                     ).then_inc(silu_made, 1)

            def hid_high(quad, n):
                step_no = BLOCKS * quad + n
                if n < BLOCKS - 1:
                    rows = P
                    act.wait_ge(hid_made, 8 * quad + n + 1)
                else:
                    rows = MID
                    act.wait_ge(prod_made, step_no + 1)
                copy(hid_hi[0:rows, place(n)], hid[0:rows, place(n)]).then_inc(hid_hi_made, 1)

            def y_out(quad):
                act.wait_ge(y_done, quad + 1)
                copy(y_t, acc[:]).then_inc(y_copied, 1)

            def quad_body(quad, first, last):
                for n in range(BLOCKS):
                    if n == LAG and not first:
                        y_out(quad - 1)
                    silu(quad, n)
                    if first and n == 0:
                        attn_out(GROUPS - 1)
                        route_out(0, score_bank[1])
                    elif n == 0:
                        route_out(quad, misc)
                    if n == 1 and not last:
                        x2_high(quad + 1, misc)
                    if n > 0:
                        hid_high(quad, n - 1)
                    elif not first:
                        hid_high(quad - 1, BLOCKS - 1)
                    if n == 3 and not last:
                        logit_silus(quad + 1)

            act.wait_ge(pv_done, 4 * PAIRS)
            act.wait_ge(sel_f_made, 1)
            copy(sel, sel_f).then_inc(sel_made, 1)
            weight_high(2)
            weight_high(3)
            logit_silus(0)
            quad_body(0, True, False)
            with act.Fori(1, QUADS - 1) as quad:
                quad_body(quad, False, False)
            quad_body(QUADS - 1, False, True)
            hid_high(QUADS - 1, BLOCKS - 1)
            y_out(QUADS - 1)

        @block.vector
        def _(dve):
            sub = lambda dst, a, b: nc.vector.tensor_tensor(dst, a, b, ALU.subtract)
            flat = lambda ap: ap.rearrange("p a b -> p (a b)")

            dve.wait_ge(mask_in, 16)
            dve.wait_ge(m_done, 4)
            nc.vector.tensor_scalar(mask_neg, mask_u8[:], -1.0, -MASKED, ALU.add, ALU.mult
                                    ).then_inc(mask_neg_made, 1)

            def wait_before(sem_, value):
                dve.wait_ge(sem_, value)
                nc.vector.memset(wait_cell[:], 0.0)

            def statistics(group):
                for k in range(2):
                    tile = flat(xall[:, bass.ds(2 * group + k, 1), :])
                    last = nc.vector.bn_stats(stats[:, k, :], tile)
                last.then_inc(ln_step, 1)
                wait_before(ln_step, 2 * group + 1)
                for k in range(2):
                    last = nc.vector.bn_aggr(mean_var[:, k, :], stats[:, k, :])
                last.then_inc(ln_step, 1)
                dve.wait_ge(ln_step, 2 * group + 2)
                nc.vector.tensor_scalar(var_eps[:, 0:2, :], mean_var[:, 0:2, 1:2], LN_EPS, None, ALU.add
                                        ).then_inc(var_made, 1)

            def layer_norm(group):
                dve.wait_ge(rstd_made, group + 1)
                at_least(dve, xt_done, group)
                for k in range(2):
                    tile = flat(xall[:, bass.ds(2 * group + k, 1), :])
                    last = nc.vector.tensor_scalar(xn[:, k, :], tile, mean_var[:, k, 0:1], rstd[:, k, :],
                                                   ALU.subtract, ALU.mult)
                last.then_inc(xn_made, 1)

            dve.wait_ge(x_first_in, 16)
            statistics(0)
            layer_norm(0)
            for c in range(4):
                dve.wait_ge(m_hi_made, c + 1)
                part = slice(4 * c, 4 * c + 4)
                sub(flat(m_lo[:, part, :]), bank[c][:], flat(m_hi[:, part, :])).then_inc(m_lo_made, 1)
            for c in range(4):
                dve.wait_ge(b_hi_made, c + 1)
                part = slice(4 * c, 4 * c + 4)
                sub(flat(b_lo[:, part, :]), bank[c][:], flat(b_hi[:, part, :])).then_inc(b_lo_made, 1)
            dve.wait_ge(consts_made, 4)
            for c in range(4):
                dve.wait_ge(mask_spread, c + 1)
                nc.vector.tensor_tensor(maskb[:, 8 * c:8 * c + 8, :],
                                        bank[4 + c][:].rearrange("p (t k) -> p t k", k=SEQ),
                                        tri[:].unsqueeze(1).to_broadcast([P, 8, SEQ]), ALU.add
                                        ).then_inc(mask_made, 1)

            def ctx_t_low(group):
                dve.wait_ge(ct_hi_made, group + 1)
                sub(ct_lo[:].rearrange("p (b k) -> p b k", k=SEQ), once(rot[1]),
                    ct_hi[:].rearrange("p (b k) -> p b k", k=SEQ)).then_inc(ct_lo_made, 1)

            def maximum(pair, half):
                dve.wait_ge(scores_done, 2 * pair + half + 1)
                nc.vector.tensor_reduce(row_max[:, 8 * half:8 * half + 8],
                                        score_bank[half][:].rearrange("p (h k) -> p h k", k=SEQ), AX_X, ALU.max
                                        ).then_inc(max_made, 1)

            def shift(pair, half):
                heads = slice(8 * half, 8 * half + 8)
                dve.wait_ge(max_made, 2 * pair + half + 1)
                if half == 0:
                    at_least(dve, pt_done, 2 * pair)
                sub(probs[:, heads, :], score_bank[half][:].rearrange("p (h k) -> p h k", k=SEQ),
                    row_max[:, heads].unsqueeze(2).to_broadcast([P, 8, SEQ])).then_inc(shifted, 1)

            def sums(pair):
                for half in range(2):
                    heads = slice(8 * half, 8 * half + 8)
                    dve.wait_ge(exp_made, 2 * pair + half + 1)
                    nc.vector.tensor_reduce(row_sum[:, heads], probs[:, heads, :], AX_X, ALU.add
                                            ).then_inc(sum_made, 1)
                nc.vector.tensor_scalar(nan_probe[:], row_max[:], 1e9, None, ALU.mult).then_inc(inv_step, 1)
                dve.wait_ge(sum_made, 2 * pair + 2)
                nc.vector.reciprocal(inv_raw[:], row_sum[:]).then_inc(inv_step, 1)
                dve.wait_ge(inv_step, 2 * pair + 2)
                at_least(dve, probs_made, 2 * pair)
                nc.vector.scalar_tensor_tensor(inv[:], nan_probe[:], 0.0, inv_raw[:], ALU.mult, ALU.add
                                               ).then_inc(inv_made, 1)

            def probs_t_low(pair, v, src):
                dve.wait_ge(pt_hi_made, 2 * pair + v + 1)
                part = slice(4 * v, 4 * v + 4)
                sub(flat(pt_lo[:, part, :]), src[:], flat(pt_hi[:, part, :])).then_inc(pt_lo_made, 1)

            def r_low(pair, s, b):
                parity, r = s // 2, s % 2
                col = r * P + b * SEQ
                for h2 in range(2):
                    dve.wait_ge(r_hi_made, 4 * pair + 2 * b + h2 + 1)
                    pick = lambda t: t[:, parity, :, col:col + SEQ].rearrange("p (n a) q -> p n a q", a=2)[:, :, h2, :]
                    sub(pick(r_lo), pv_bank[h2][:].rearrange("p (n q) -> p n q", q=SEQ), pick(r_hi)
                        ).then_inc(r_lo_made, 1)

            def add_attn(group, src):
                dve.wait_ge(attn_turned, group + 1)
                tiles = xall[:, bass.ds(2 * group, 2), :]
                nc.vector.tensor_tensor(tiles, src[:, 0:GT].rearrange("p (t d) -> p t d", d=P), tiles, ALU.add
                                        ).then_inc(x2_made, 1)

            def statistics2(group):
                wait_before(x2_made, group + 1)
                for k in range(2):
                    last = nc.vector.bn_stats(stats2[:, k, :], flat(xall[:, bass.ds(2 * group + k, 1), :]))
                last.then_inc(ln2_step, 1)
                wait_before(ln2_step, 2 * group + 1)
                for k in range(2):
                    last = nc.vector.bn_aggr(mean_var2[:, k, :], stats2[:, k, :])
                last.then_inc(ln2_step, 1)
                dve.wait_ge(ln2_step, 2 * group + 2)
                nc.vector.tensor_copy(mean2[:, bass.ds(2 * group, 2), :], mean_var2[:, :, 0:1])
                nc.vector.tensor_scalar(var_eps2[:, bass.ds(2 * group, 2), :], mean_var2[:, :, 1:2],
                                        LN_EPS, None, ALU.add).then_inc(var2_made, 1)

            def layer_norm2(quad):
                at_least(dve, x2t_done, quad)
                for k in range(4):
                    last = nc.vector.tensor_scalar(xn2[:, k, :], flat(xall[:, bass.ds(4 * quad + k, 1), :]),
                                                   flat(mean2[:, bass.ds(4 * quad + k, 1), :]),
                                                   flat(rstd2[:, bass.ds(4 * quad + k, 1), :]),
                                                   ALU.subtract, ALU.mult)
                last.then_inc(xn2_made, 1)

            ctx_t_low(0)
            statistics(1)
            layer_norm(1)
            ctx_t_low(1)
            for half in range(2):
                maximum(0, half)
                shift(0, half)
            sums(0)
            dve.wait_ge(x_rest_in, 16)

            def body(i, first, last):
                for s in range(4):
                    pair, parity, r = 4 * i + s, s // 2, s % 2
                    group = 2 * i + parity
                    more = not (last and s == 3)
                    if more:
                        maximum(pair + 1, 0)
                        maximum(pair + 1, 1)
                    turned = (rot[0], rot[1]) if r == 0 else (rot[2], rot[0])
                    probs_t_low(pair, 0, turned[0])
                    probs_t_low(pair, 1, turned[1])
                    if last and s == 3:
                        dve.wait_ge(pt_done, 2 * PAIRS)
                        dve.wait_ge(rstd2_made, 1)
                        layer_norm2(0)
                    if more:
                        shift(pair + 1, 0)
                        shift(pair + 1, 1)
                        sums(pair + 1)
                    r_low(pair, s, 0)
                    if r == 0 and not last:
                        ctx_t_low(group + 2)
                    if r == 1 and not first:
                        add_attn(group - 2, rot[2])
                    if r == 1 and not last:
                        layer_norm(group + 2)
                    r_low(pair, s, 1)
                    if r == 0 and not last:
                        statistics(group + 2)
                    if r == 1 and not first and not (last and s == 3):
                        statistics2(group - 2)

            body(0, True, False)
            with dve.Fori(1, BODIES - 1) as i:
                body(i, False, False)
            body(BODIES - 1, False, True)

            up_bank, spread_bank, misc = bank[2:4], bank[4:6], bank[6]
            dve.wait_ge(fill_made, 4)

            def fix_logits(quad, src):
                z = src[:, 0:4 * EXPERTS].rearrange("p (t e) -> p t e", e=EXPERTS)
                dve.wait_ge(logit_done, quad + 1)
                nc.vector.tensor_scalar(logit_fix[:], z, 0.0, 1e-20, ALU.is_equal, ALU.mult).then_inc(logit_step, 1)
                dve.wait_ge(logit_step, 2 * quad + 1)
                at_least(dve, silu_of_logit, quad)
                nc.vector.scalar_tensor_tensor(logit[:], z, SATURATED, logit_fix[:], ALU.min, ALU.add
                                               ).then_inc(logit_made, 1)
                dve.wait_ge(logit_made, quad + 1)
                nc.vector.reciprocal(logit_inv[:], logit[:]).then_inc(logit_step, 1)

            def pick_experts(quad):
                t0 = 8 * quad
                dve.wait_ge(silu_of_logit, quad + 1)
                dve.wait_ge(logit_step, 2 * quad + 2)
                real = score[:, :, 0:EXPERTS]
                nc.vector.tensor_tensor(real, logit_silu[:], logit_inv[:], ALU.mult).then_inc(top_step, 1)
                wait_before(top_step, t0 + 1)
                for k in range(4):
                    last = nc.vector.max(best[:, k, :], score[:, k, :])
                last.then_inc(top_step, 1)
                dve.wait_ge(top_step, t0 + 2)
                nc.vector.tensor_copy(taken[:, :, 0:2], best[:, :, 0:2]).then_inc(top_step, 1)
                nc.vector.tensor_tensor(best_sum[:], best[:, :, 0:1], best[:, :, 1:2], ALU.add).then_inc(top_step, 1)

            def mark_experts(quad):
                t0 = 8 * quad
                real = score[:, :, 0:EXPERTS]
                wait_before(top_step, t0 + 4)
                for k in range(4):
                    last = nc.vector.match_replace(marked[:, k, :], taken[:, k, :], score[:, k, :], -5.0)
                last.then_inc(top_step, 1)
                nc.vector.tensor_scalar(best_sum[:], best_sum[:], 1e-20, None, ALU.add).then_inc(top_step, 1)
                dve.wait_ge(top_step, t0 + 6)
                nc.vector.reciprocal(best_inv[:], best_sum[:]).then_inc(top_step, 1)
                nc.vector.scalar_tensor_tensor(picked[:], marked[:, :, 0:EXPERTS], -3.0, real, ALU.is_lt, ALU.mult
                                               ).then_inc(top_step, 1)
                dve.wait_ge(top_step, t0 + 8)

            def split_route(quad):
                nc.vector.scalar_tensor_tensor(route[:], picked[:], TOP_SCALE,
                                               best_inv[:].to_broadcast([P, 4, EXPERTS]), ALU.mult, ALU.mult
                                               ).then_inc(route_step, 1)
                dve.wait_ge(route_step, 2 * quad + 1)
                at_least(dve, route_turned, quad)
                nc.vector.tensor_copy(route2[:, :, 0:EXPERTS], route[:]).then_inc(route_step, 1)
                dve.wait_ge(route_step, 2 * quad + 2)
                sub(route2[:, :, EXPERTS:2 * EXPERTS], route[:], route2[:, :, 0:EXPERTS]).then_inc(route_made, 1)

            def product(quad, n):
                step_no = BLOCKS * quad + n
                dve.wait_ge(silu_made, step_no + 1)
                at_least(dve, hid_lo_made, step_no - 3)
                if n < BLOCKS - 1:
                    dve.wait_ge(up_done, 8 * quad + n + 1)
                    nc.vector.tensor_tensor(hid[:, place(n)], up_bank[n % 2][:], sg[:, n % 3], ALU.mult
                                            ).then_inc(prod_made, 1)
                    dve.wait_ge(prod_made, step_no + 1)
                    nc.vector.tensor_tensor(hid[:, place(n)], spread_bank[n % 2][:], hid[:, place(n)], ALU.mult
                                            ).then_inc(hid_made, 1)
                else:
                    nc.vector.tensor_tensor(hid[0:MID, place(n)], spread_bank[0][MID:P, :], sg[0:MID, n % 3], ALU.mult
                                            ).then_inc(prod_made, 1)

            def add_experts(quad):
                dve.wait_ge(y_turned, quad + 1)
                at_least(dve, out_stored, 16 * quad)
                nc.vector.tensor_tensor(out_sb, misc[:].rearrange("p (t d) -> p t d", d=P),
                                        xall[:, bass.ds(4 * quad, 4), :], ALU.add).then_inc(out_made, 1)

            def quad_body(quad, first, last):
                for n in range(BLOCKS):
                    if n == 0 and not last:
                        layer_norm2(quad + 1)
                    product(quad, n)
                    if first and n == 1:
                        add_attn(GROUPS - 1, acc[:, GT:2 * GT])
                    if first and n in (2, 3, 4):
                        statistics2(GROUPS - 5 + n)
                    if n == 3 and not last:
                        fix_logits(quad + 1, misc)
                    if n == 4 and not last:
                        pick_experts(quad + 1)
                    if n == 6 and not last:
                        mark_experts(quad + 1)
                    if n == 7 and not last:
                        split_route(quad + 1)
                    if n == 5 and not first:
                        add_experts(quad - 1)

            fix_logits(0, score_bank[0])
            pick_experts(0)
            add_attn(GROUPS - 2, rot[1])
            mark_experts(0)
            split_route(0)
            quad_body(0, True, False)
            dve.wait_ge(rstd2_made, 2)
            with dve.Fori(1, QUADS - 1) as quad:
                quad_body(quad, False, False)
            quad_body(QUADS - 1, False, True)
            add_experts(QUADS - 1)


_INS = ['x', 'ctx_1024', 'mask_BxS2_bf1', 'L0_xattn_Wq', 'L0_xattn_Wk', 'L0_xattn_Wv', 'L0_xattn_Wo', 'L0_xattn_bo',
        'L0_ffn_gate_w', 'L0_ffn_w_gate', 'L0_ffn_w_up', 'L0_ffn_w_down', 'L0_ffn_ws_gate', 'L0_ffn_ws_up',
        'L0_ffn_ws_down']


def kernel(**inputs):
    import numpy as _np
    import concourse.bacc as _bacc
    from concourse import mybir as _mybir
    from concourse.bass_utils import run_bass_kernel_spmd as _run

    nc = _bacc.Bacc("TRN2", target_bir_lowering=False, num_devices=1)
    arrays, args = {}, []
    for name in _INS:
        a = _np.ascontiguousarray(inputs[name])
        if a.dtype == _np.bool_:
            a = a.view(_np.uint8)
        arrays[f"in_{name}"] = a
        args.append(nc.dram_tensor(f"in_{name}", a.shape, _mybir.dt.from_np(a.dtype), kind="ExternalInput").ap())
    shape = inputs['x'].shape
    args.append(nc.dram_tensor("out_x", tuple(shape), _mybir.dt.float32, kind="ExternalOutput").ap())
    xattn_moe_kernel(nc, *args)
    r = _run(nc, [arrays], core_ids=[0])
    return r.results[0]["out_x"]
```

```python
from contextlib import ExitStack

import concourse.bass as bass
from concourse import mybir

F32 = mybir.dt.float32
F32R = mybir.dt.float32r
BF16 = mybir.dt.bfloat16
ALU = mybir.AluOpType
ACT = mybir.ActivationFunctionType
AX_X = mybir.AxisListType.X

P = 128
HEADS = 16
HD = 64
SEQ = 64
EXPERTS = 16
MID = 64
TOP_SCALE = 2.5
LN_EPS = 1e-5
SATURATED = 20.0
MASKED = -1e30


def at_least(eng, sem, value):
    if isinstance(value, int) and value <= 0:
        return
    eng.wait_ge(sem, value)


def xattn_moe_kernel(nc, x, ctx_in, mask, Wq, Wk, Wv, Wo, bo, gate_w, w_gate, w_up, w_down,
                     ws_gate, ws_up, ws_down, out):
    batches = x.shape[0]
    PAIRS = batches // 2
    BODIES = PAIRS // 4
    GROUPS = PAIRS // 2
    GT = 2 * P
    BLOCKS = EXPERTS // 2 + 1
    QUADS = PAIRS // 4
    WARM_UP = 12
    LAG = 3
    QT = 4 * P

    x_tiles = x.rearrange("(t b) s d -> (t b s) d", b=2).rearrange("(t p) d -> p t d", p=P)
    out_tiles = out.rearrange("(t b) s d -> (t b s) d", b=2).rearrange("(t p) d -> p t d", p=P)

    with ExitStack() as stack:
        def sb(name, shape, dt=F32):
            return stack.enter_context(nc.sbuf_tensor(name, shape, dt))

        def sem(name):
            return stack.enter_context(nc.semaphore(name))

        bank = [stack.enter_context(nc.psum_tensor(f"bank{i}", [P, 512], F32)) for i in range(8)]
        rot = bank[0:3]
        score_bank = bank[3:5]
        pv_bank = bank[5:7]
        acc = bank[7]
        b_bank = [pv_bank[0], pv_bank[1], acc, rot[2]]

        xall = sb("xall", [P, PAIRS, P])
        keys = sb("keys", [P, 2, HEADS, GT])
        r_hi = sb("r_hi", [P, 2, HEADS, GT], F32R)
        r_lo = sb("r_lo", [P, 2, HEADS, GT], F32R)
        pt_hi = sb("pt_hi", [P, 8, P], F32R)
        pt_lo = sb("pt_lo", [P, 8, P], F32R)
        probs = sb("probs", [P, HEADS, SEQ])
        craw = sb("craw", [P, 2, 4, P])
        c_hi = sb("c_hi", [P, 2, 4, P], F32R)
        c_lo = sb("c_lo", [P, 2, 4, P], F32R)
        ct_hi = sb("ct_hi", [P, GT], F32R)
        ct_lo = sb("ct_lo", [P, GT], F32R)
        xt = sb("xt", [P, 2, GT])
        xn = sb("xn", [P, 2, P])
        attn_t = sb("attn_t", [P, GT])
        m_hi = sb("m_hi", [P, HEADS, P], F32R)
        m_lo = sb("m_lo", [P, HEADS, P], F32R)
        b_hi = sb("b_hi", [P, HEADS, P], F32R)
        b_lo = sb("b_lo", [P, HEADS, P], F32R)
        wg_hi = sb("wg_hi", [P, BLOCKS, P], F32R)
        wg_lo = sb("wg_lo", [P, BLOCKS, P], F32R)
        wu_hi = sb("wu_hi", [P, BLOCKS - 1, P], F32R)
        wu_lo = sb("wu_lo", [P, BLOCKS - 1, P], F32R)
        maskb = sb("maskb", [P, PAIRS, SEQ], BF16)
        tri = sb("tri", [P, SEQ])
        ident = sb("ident", [P, P])
        ident_b = sb("ident_b", [P, P], BF16)
        mask_u8 = sb("mask_u8", [2, PAIRS, SEQ], mask.dtype)
        half_of = sb("half_of", [2, P], BF16)
        bo_col = sb("bo_col", [P, 1])
        gw_row = sb("gw_row", [EXPERTS, P])
        gw_t = sb("gw_t", [P, EXPERTS])
        wait_cell = sb("wait_cell", [P, 1])
        zero_col = sb("zero_col", [P, 1])
        stats = sb("stats", [P, 2, 6])
        mean_var = sb("mean_var", [P, 2, 2])
        var_eps = sb("var_eps", [P, 2, 1])
        rstd = sb("rstd", [P, 2, 1])
        stats2 = sb("stats2", [P, 2, 6])
        mean_var2 = sb("mean_var2", [P, 2, 2])
        moments2 = sb("moments2", [P, PAIRS, 2])
        var_eps2 = sb("var_eps2", [P, PAIRS, 1])
        rstd2 = sb("rstd2", [P, PAIRS, 1])
        minus_half = sb("minus_half", [P, 1, 1])
        row_max = sb("row_max", [P, HEADS])
        row_sum = sb("row_sum", [P, HEADS])
        nan_probe = sb("nan_probe", [P, HEADS])
        inv_raw = sb("inv_raw", [P, HEADS])
        inv = sb("inv", [P, HEADS])
        score = sb("score", [P, 4, EXPERTS + 8])
        best = sb("best", [P, 4, 8])
        taken = sb("taken", [P, 4, 8])
        marked = sb("marked", [P, 4, EXPERTS + 8])
        best_sum = sb("best_sum", [P, 4, 1])
        best_inv = sb("best_inv", [P, 4, 1])
        picked = sb("picked", [P, 4, EXPERTS])
        route = sb("route", [P, 4, EXPERTS])
        route2 = sb("route2", [P, 4, 2 * EXPERTS], F32R)

        keys_flat = keys[:].rearrange("p a h t -> p (a h t)")
        by_two = lambda ap: ap.rearrange("p (n e) -> p n e", e=P)
        wq_s, wk_s = by_two(keys_flat[:, 0:1024]), by_two(keys_flat[:, 1024:2048])
        late_x = xall[:, 8:PAIRS, :].rearrange("p t d -> p (t d)")
        wv_s, wo_t, wo_s = by_two(late_x[:, 0:1024]), by_two(late_x[:, 1024:2048]), late_x[:, 2048:3072]
        mask_neg = probs[:].rearrange("p h k -> p (h k)")[0:2, :].bitcast(BF16).rearrange("b (t k) -> b t k", k=SEQ)
        heads_of = lambda c: range(8 * (c // 2) + c % 2, 8 * (c // 2) + 8, 2)
        four_heads = lambda w, c: w[:, 8 * (c // 2):8 * (c // 2) + 8, :].rearrange(
            "p (n a) e -> p n a e", a=2)[:, :, c % 2, :]
        of_head = lambda w, h: w[(h % 2) * HD:(h % 2 + 1) * HD, h // 2, :]
        craw_flat = craw[:].rearrange("p a b e -> p (a b e)")
        sel_f = craw_flat[0:2 * EXPERTS, :].rearrange("p (n r) -> p n r", n=8)
        sel = pt_lo[0:2 * EXPERTS]
        route_t = pt_hi[0:2 * EXPERTS, 0:4, :].rearrange("p n t -> p (n t)")
        wg_raw = keys_flat[:, 0:1152]
        wu_raw = keys_flat[:, 1152:2176]
        wd_raw = keys_flat[:, 2176:3328]
        sg = keys_flat[:, 4096:5632].rearrange("p (n t) -> p n t", n=3)
        hid = keys_flat[:, 5632:8192].rearrange("p (n t) -> p n t", n=5)
        place = lambda n: n % 4 if n < BLOCKS - 1 else 4
        y_t = craw_flat[:, 0:QT]
        out_sb = craw_flat[:, QT:2 * QT].rearrange("p (n d) -> p n d", n=4)
        logit_fix, logit, logit_inv, logit_silu = [
            xn[:].rearrange("p k e -> p (k e)")[:, 64 * k:64 * k + 64].rearrange("p (t e) -> p t e", e=EXPERTS)
            for k in range(4)]
        wd_hi = m_hi[:, 0:BLOCKS, :]
        wd_lo = m_lo[:, 0:BLOCKS, :]
        rh_flat = r_hi[:].rearrange("p a h t -> p (a h t)")
        rl_flat = r_lo[:].rearrange("p a h t -> p (a h t)")
        x2_hi = rh_flat[:, 0:4096].rearrange("p (g t) -> p g t", g=QUADS)
        x2_lo = rl_flat[:, 0:4096].rearrange("p (g t) -> p g t", g=QUADS)
        hid_hi = rh_flat[:, 4096:6656].rearrange("p (n t) -> p n t", n=5)
        hid_lo = rl_flat[:, 4096:6656].rearrange("p (n t) -> p n t", n=5)
        probs_flat = probs[:].rearrange("p h k -> p (h k)")
        x2_f = probs_flat[:, 0:QT]
        xn2 = probs_flat[:, QT:2 * QT].rearrange("p (n d) -> p n d", n=4)

        flat3 = lambda ap: ap.rearrange("p n d -> p (n d)")
        ffn_parts = [(flat3(wg_hi[:]), flat3(wg_lo[:]), wg_raw), (flat3(wu_hi[:]), flat3(wu_lo[:]), wu_raw),
                     (flat3(wd_hi[:, 0:8, :]), flat3(wd_lo[:, 0:8, :]), wd_raw[:, 0:1024]),
                     (wd_hi[0:MID, 8, :], wd_lo[0:MID, 8, :], wd_raw[0:MID, 1024:1152])]

        wk_in, wo_in, x_first_in, x_rest_in = sem("wk_in"), sem("wo_in"), sem("x_first_in"), sem("x_rest_in")
        x_late_in = sem("x_late_in")
        wv_in, mask_in, small_in, ffn_in = sem("wv_in"), sem("mask_in"), sem("small_in"), sem("ffn_in")
        ctx_landed = [sem("ctx_even_in"), sem("ctx_odd_in")]
        pool_step, consts_made = sem("pool_step"), sem("consts_made")
        sel_made, mask_neg_made = sem("sel_made"), sem("mask_neg_made")
        m_done, m_hi_made, m_lo_made = sem("m_done"), sem("m_hi_made"), sem("m_lo_made")
        wot_done, wot_copied = sem("wot_done"), sem("wot_copied")
        b_done, b_hi_made, b_lo_made = sem("b_done"), sem("b_hi_made"), sem("b_lo_made")
        mask_spread, mask_made = sem("mask_spread"), sem("mask_made")
        ctx_hi_made, ctx_lo_made = sem("ctx_hi_made"), sem("ctx_lo_made")
        ct_done, ct_hi_made, ct_lo_made = sem("ct_done"), sem("ct_hi_made"), sem("ct_lo_made")
        keys_done, keys_copied = sem("keys_done"), sem("keys_copied")
        ln_step, var_made, rstd_made = sem("ln_step"), sem("var_made"), sem("rstd_made")
        x_centred, xn_made, xt_done, xt_copied = sem("x_centred"), sem("xn_made"), sem("xt_done"), sem("xt_copied")
        scores_done, masked, max_made = sem("scores_done"), sem("masked"), sem("max_made")
        shifted, exp_made = sem("shifted"), sem("exp_made")
        sum_made, inv_step, inv_made, probs_made = sem("sum_made"), sem("inv_step"), sem("inv_made"), sem("probs_made")
        pt_done, pt_hi_made, pt_lo_made = sem("pt_done"), sem("pt_hi_made"), sem("pt_lo_made")
        pv_done, r_hi_made, r_lo_made = sem("pv_done"), sem("r_hi_made"), sem("r_lo_made")
        attn_done, attn_copied, attn_turned, x2_made = sem("attn_done"), sem("attn_copied"), sem("attn_turned"), sem("x2_made")
        ffn_hi_made, ffn_lo_made = sem("ffn_hi_made"), sem("ffn_lo_made")
        gwt_done, gwt_copied = sem("gwt_done"), sem("gwt_copied")
        sel_f_made = sem("sel_f_made")
        ln2_step, var2_made, rstd2_made = sem("ln2_step"), sem("var2_made"), sem("rstd2_made")
        xn2_made, x2t_done = sem("xn2_made"), sem("x2t_done")
        x2_f_made, x2_lo_made = sem("x2_f_made"), sem("x2_lo_made")
        logit_done, logit_step, logit_made, silu_of_logit = sem("logit_done"), sem("logit_step"), sem("logit_made"), sem("silu_of_logit")
        top_step, route_made, route_turned, route_copied = sem("top_step"), sem("route_made"), sem("route_turned"), sem("route_copied")
        fill_made, route_step = sem("fill_made"), sem("route_step")
        gate_done, up_done, silu_made, hid_made = sem("gate_done"), sem("up_done"), sem("silu_made"), sem("hid_made")
        prod_made, hid_hi_made, hid_lo_made = sem("prod_made"), sem("hid_hi_made"), sem("hid_lo_made")
        y_done, y_copied, y_turned, out_made, out_stored = sem("y_done"), sem("y_copied"), sem("y_turned"), sem("out_made"), sem("out_stored")

        block = stack.enter_context(nc.Block())

        def once(bank_):
            return bank_[:].rearrange("p (b a k) -> p b a k", a=2, k=SEQ)[:, :, 0, :]

        @block.sync
        def _(sp):
            def load_ctx(group, parity):
                for half in range(2):
                    sp.dma_start(craw[half * SEQ:(half + 1) * SEQ, parity],
                                 ctx_in[bass.ds(4 * group, 4)].rearrange("b k e -> k b e")
                                 ).then_inc(ctx_landed[parity], 16)

            sp.dma_start(wk_s, Wk.rearrange("(n p) e -> p n e", p=P)).then_inc(wk_in, 16)
            sp.dma_start(wq_s, Wq.rearrange("(n p) e -> p n e", p=P)).then_inc(wk_in, 16)
            load_ctx(0, 0)
            sp.dma_start(wo_s, Wo).then_inc(wo_in, 16)
            sp.dma_start(wv_s, Wv.rearrange("(n p) e -> p n e", p=P)).then_inc(wv_in, 16)
            load_ctx(1, 1)
            sp.dma_start(bo_col[:], bo.rearrange("(d a) -> d a", a=1)).then_inc(small_in, 16)
            sp.dma_start(gw_row[:], gate_w).then_inc(small_in, 16)
            sp.dma_start(xall[:, 4:8, :], x_tiles[:, 4:8, :]).then_inc(x_rest_in, 16)
            sp.wait_ge(b_done, 4)
            sp.dma_start(xall[:, 8:PAIRS, :], x_tiles[:, 8:PAIRS, :]).then_inc(x_late_in, 16)

            def body(i, last):
                for parity in range(2):
                    if last:
                        continue
                    group = 2 * i + parity
                    sp.wait_ge(ctx_lo_made, group + 1)
                    sp.wait_ge(ct_done, group + 1)
                    load_ctx(group + 2, parity)

            with sp.Fori(0, BODIES - 1) as i:
                body(i, False)

            sp.wait_ge(scores_done, 2 * (PAIRS - 2))
            sp.dma_start(wg_raw[:, 0:1024].rearrange("p (e m) -> p e m", m=MID),
                         w_gate.rearrange("e h m -> h e m")).then_inc(ffn_in, 16)
            sp.dma_start(wg_raw[:, 1024:1088], ws_gate).then_inc(ffn_in, 16)
            sp.dma_start(wg_raw[:, 1088:1152], ws_up).then_inc(ffn_in, 16)
            sp.dma_start(wu_raw.rearrange("p (e m) -> p e m", m=MID),
                         w_up.rearrange("e h m -> h e m")).then_inc(ffn_in, 16)
            sp.dma_start(wd_raw[:, 0:1024].rearrange("p (n d) -> p n d", d=P),
                         w_down.rearrange("(n a) m d -> (a m) n d", a=2)).then_inc(ffn_in, 16)
            sp.dma_start(wd_raw[0:MID, 1024:1152], ws_down).then_inc(ffn_in, 16)

            with sp.Fori(0, QUADS) as quad:
                sp.wait_ge(out_made, quad + 1)
                sp.dma_start(out_tiles[:, bass.ds(4 * quad, 4), :], out_sb).then_inc(out_stored, 16)
            sp.wait_ge(out_stored, 16 * QUADS)

        @block.gpsimd
        def _(pool):
            steps = [0]

            def step(ins):
                steps[0] += 1
                ins.then_inc(pool_step, 1)
                pool.wait_ge(pool_step, steps[0])

            step(nc.gpsimd.memset(ident[:], 0.0))
            step(nc.gpsimd.affine_select(out=ident[:], in_=ident[:], compare_op=ALU.not_equal, fill=1.0,
                                         base=0, pattern=[[-1, P]], channel_multiplier=1))
            nc.gpsimd.tensor_copy(ident_b[:], ident[:]).then_inc(consts_made, 1)
            step(nc.gpsimd.memset(tri[:], 0.0))
            for half in range(2):
                rows = tri[half * SEQ:(half + 1) * SEQ, :]
                nc.gpsimd.affine_select(out=rows, in_=rows, compare_op=ALU.is_ge, fill=MASKED, base=0,
                                        pattern=[[-1, SEQ]], channel_multiplier=1).then_inc(consts_made, 1)
            step(nc.gpsimd.memset(half_of[:], 1.0))
            step(nc.gpsimd.affine_select(out=half_of[:], in_=half_of[:], compare_op=ALU.is_ge, fill=0.0,
                                         base=0, pattern=[[1, P]], channel_multiplier=-SEQ))
            nc.gpsimd.affine_select(out=half_of[:], in_=half_of[:], compare_op=ALU.is_ge, fill=0.0,
                                    base=SEQ - 1, pattern=[[-1, P]], channel_multiplier=SEQ).then_inc(consts_made, 1)

            def split_ctx(group, parity, round_):
                at_least(pool, pv_done, 8 * (group - 1))
                pool.wait_ge(ctx_landed[parity], 32 * (round_ + 1))
                nc.gpsimd.tensor_tensor(c_hi[:, parity], craw[:, parity],
                                        zero_col[:].unsqueeze(1).to_broadcast([P, 4, P]), ALU.add
                                        ).then_inc(ctx_hi_made, 1)
                pool.wait_ge(ctx_hi_made, group + 1)
                nc.gpsimd.tensor_tensor(c_lo[:, parity], craw[:, parity], c_hi[:, parity],
                                        ALU.subtract).then_inc(ctx_lo_made, 1)

            def shift(pair):
                for half in range(2):
                    heads = slice(8 * half, 8 * half + 8)
                    pool.wait_ge(max_made, 2 * pair + half + 1)
                    nc.gpsimd.tensor_tensor(probs[:, heads, :], probs[:, heads, :],
                                            row_max[:, heads].unsqueeze(2).to_broadcast([P, 8, SEQ]),
                                            ALU.subtract).then_inc(shifted, 1)

            def normalise(pair):
                pool.wait_ge(inv_made, pair + 1)
                for half in range(2):
                    heads = slice(8 * half, 8 * half + 8)
                    nc.gpsimd.tensor_tensor(probs[:, heads, :], probs[:, heads, :],
                                            inv[:, heads].unsqueeze(2).to_broadcast([P, 8, SEQ]),
                                            ALU.mult).then_inc(probs_made, 1)

            nc.gpsimd.memset(minus_half[:], -0.5).then_inc(fill_made, 1)
            nc.gpsimd.memset(zero_col[:], 0.0).then_inc(fill_made, 1)
            pool.wait_ge(fill_made, 2)

            def deviation(group):
                pool.wait_ge(var_made, group + 1)
                nc.gpsimd.tensor_tensor(rstd[:], var_eps[:], minus_half[:].to_broadcast([P, 2, 1]), ALU.pow
                                        ).then_inc(rstd_made, 1)

            def layer_norm(group):
                at_least(pool, xt_done, group)
                tiles = xall[:, bass.ds(2 * group, 2), :]
                pool.wait_ge(rstd_made, group + 1)
                nc.gpsimd.tensor_tensor(xn[:], tiles, mean_var[:, :, 0:1].to_broadcast([P, 2, P]), ALU.subtract
                                        ).then_inc(x_centred, 1)
                pool.wait_ge(x_centred, group + 1)
                nc.gpsimd.tensor_tensor(xn[:], xn[:], rstd[:].to_broadcast([P, 2, P]), ALU.mult
                                        ).then_inc(xn_made, 1)

            def deviation2(groups):
                pool.wait_ge(var2_made, groups.stop)
                tiles = slice(2 * groups.start, 2 * groups.stop)
                step(nc.gpsimd.tensor_scalar(var_eps2[:, tiles, :], moments2[:, tiles, 1:2], LN_EPS, None, ALU.add))
                nc.gpsimd.tensor_tensor(rstd2[:, tiles, :], var_eps2[:, tiles, :],
                                        minus_half[:].to_broadcast([P, 2 * len(groups), 1]), ALU.pow
                                        ).then_inc(rstd2_made, 1)

            deviation(0)
            layer_norm(0)
            split_ctx(0, 0, 0)
            deviation(1)
            layer_norm(1)
            split_ctx(1, 1, 0)
            nc.gpsimd.memset(score[:], -1.0).then_inc(fill_made, 1)
            nc.gpsimd.memset(taken[:], -1.0).then_inc(fill_made, 1)
            shift(0)
            normalise(0)

            def body(i, last):
                for s in range(4):
                    pair, parity = 4 * i + s, s // 2
                    if not (last and s >= 1):
                        shift(pair + 1)
                    if s % 2 == 1 and not last:
                        deviation(2 * i + parity + 2)
                        layer_norm(2 * i + parity + 2)
                    if last and s == 1:
                        deviation2(range(0, GROUPS - 4))
                    if not (last and s >= 1):
                        normalise(pair + 1)
                    if s % 2 == 1 and not last:
                        split_ctx(2 * i + parity + 2, parity, i + 1)
                    if last and s == 0:
                        spread_ones()

            def spread_ones():
                pool.wait_ge(ctx_lo_made, GROUPS)
                pool.wait_ge(ct_done, GROUPS)
                step(nc.gpsimd.memset(sel_f, 0.0))
                for first_row in (0, EXPERTS):
                    ins = nc.gpsimd.affine_select(out=sel_f, in_=sel_f, compare_op=ALU.not_equal, fill=1.0,
                                                  base=-first_row, pattern=[[-2, 8], [-1, 2], [0, MID]],
                                                  channel_multiplier=1)
                    if first_row == 0:
                        step(ins)
                    else:
                        ins.then_inc(sel_f_made, 1)

            with pool.Fori(0, BODIES - 1) as i:
                body(i, False)
            body(BODIES - 1, True)

            def weight_low(k):
                hi, lo, raw = ffn_parts[k]
                pool.wait_ge(ffn_hi_made, k + 1)
                nc.gpsimd.tensor_tensor(lo, raw, hi, ALU.subtract).then_inc(ffn_lo_made, 1)

            def x2_low(quad):
                pool.wait_ge(x2_f_made, quad + 1)
                nc.gpsimd.tensor_tensor(x2_lo[:, bass.ds(quad, 1), :].rearrange("p a t -> p (a t)"), x2_f,
                                        x2_hi[:, bass.ds(quad, 1), :].rearrange("p a t -> p (a t)"),
                                        ALU.subtract).then_inc(x2_lo_made, 1)

            def hid_low(quad, n):
                rows = P if n < BLOCKS - 1 else MID
                step_no = BLOCKS * quad + n
                pool.wait_ge(hid_hi_made, step_no + 1)
                at = place(n)
                nc.gpsimd.tensor_tensor(hid_lo[0:rows, at], hid[0:rows, at], hid_hi[0:rows, at],
                                        ALU.subtract).then_inc(hid_lo_made, 1)

            def quad_body(quad, first, last):
                for n in range(BLOCKS - LAG if last else BLOCKS):
                    hid_low(quad, n)
                    if n == 1 and not last:
                        x2_low(quad + 1)
                    if n == 5 and first:
                        deviation2(range(GROUPS - 4, GROUPS))

            weight_low(0)
            weight_low(1)
            x2_low(0)
            weight_low(2)
            weight_low(3)
            quad_body(0, True, False)
            with pool.Fori(1, QUADS - 1) as quad:
                quad_body(quad, False, False)
            quad_body(QUADS - 1, False, True)

        @block.tensor
        def _(pe):
            def three(out_, a_hi, a_lo, b_hi_, b_lo_, start=True, stop=True):
                nc.tensor.matmul(out_, a_hi, b_hi_, start=start, stop=False)
                nc.tensor.matmul(out_, a_lo, b_hi_, start=False, stop=False)
                return nc.tensor.matmul(out_, a_hi, b_lo_, start=False, stop=stop)

            pe.wait_ge(consts_made, 1)
            for _ in range(WARM_UP):
                nc.tensor.matmul(acc[:], ident_b[:], ident_b[:].unsqueeze(1).to_broadcast([P, 4, P]),
                                 start=True, stop=True)
            pe.wait_ge(consts_made, 4)
            pe.wait_ge(mask_neg_made, 1)
            for c in range(4):
                nc.tensor.matmul(bank[c][:], half_of[:],
                                 mask_neg.rearrange("b t k -> b (t k)")[:, 512 * c:512 * c + 512],
                                 start=True, stop=True).then_inc(mask_spread, 1)
            pe.wait_ge(wk_in, 32)
            for c in range(4):
                for k, h in enumerate(heads_of(c)):
                    last = nc.tensor.matmul(bank[4 + c][:, k * P:(k + 1) * P], of_head(wk_s, h),
                                            of_head(wq_s, h), start=True, stop=True)
                last.then_inc(m_done, 1)

            def turn_ctx(group, parity, round_):
                pe.wait_ge(ctx_landed[parity], 32 * (round_ + 1))
                for b in range(4):
                    last = nc.tensor.transpose(rot[1][:, b * P:(b + 1) * P], craw[:, parity, b, :], ident[:])
                last.then_inc(ct_done, 1)

            def turn_x(group, into):
                pe.wait_ge(xn_made, group + 1)
                for k in range(2):
                    last = nc.tensor.transpose(into[:, k * P:(k + 1) * P], xn[:, k, :], ident[:])
                last.then_inc(xt_done, 1)

            def project_keys(j, into):
                for a in range(2):
                    h = 2 * j + a
                    last = three(into[:, a * GT:(a + 1) * GT], m_hi[:, h, :], m_lo[:, h, :], ct_hi[:], ct_lo[:])
                last.then_inc(keys_done, 1)

            def scores(pair, s):
                parity, r = s // 2, s % 2
                for half in range(2):
                    at_least(pe, masked, 2 * (pair - 1) + half + 1)
                    for b in range(2):
                        col = r * P + b * SEQ
                        last = nc.tensor.matmul(score_bank[half][b * SEQ:(b + 1) * SEQ, :],
                                                xt[:, parity, col:col + SEQ],
                                                keys[:, parity, 8 * half:8 * half + 8, col:col + SEQ],
                                                start=True, stop=True)
                    last.then_inc(scores_done, 1)

            def turn_probs(pair, v, into):
                pe.wait_ge(probs_made, 2 * pair + v + 1)
                for k in range(4):
                    src = probs[:, 8 * v + 2 * k:8 * v + 2 * k + 2, :].rearrange("p h k -> p (h k)")
                    last = nc.tensor.transpose(into[:, k * P:(k + 1) * P], src, ident[:])
                last.then_inc(pt_done, 1)

            def probs_by_ctx(pair, s, b):
                parity, r = s // 2, s % 2
                for part in range(3):
                    w = c_lo if part == 1 else c_hi
                    m = pt_lo if part == 2 else pt_hi
                    for h2 in range(2):
                        if part == 0:
                            at_least(pe, r_lo_made, 4 * pair + 2 * b + h2 - 1)
                        rows = slice(h2 * SEQ, (h2 + 1) * SEQ)
                        last = nc.tensor.matmul(pv_bank[h2][:], w[rows, parity, 2 * r + b, :],
                                                m[rows, :, b * SEQ:(b + 1) * SEQ],
                                                start=(part == 0), stop=(part == 2))
                        if part == 2:
                            last.then_inc(pv_done, 1)

            def add_heads(group, parity, heads):
                for h in heads:
                    last = three(acc[:, 0:GT], b_hi[:, h, :], b_lo[:, h, :], r_hi[:, parity, h, :],
                                 r_lo[:, parity, h, :], start=(h == 0), stop=(h == HEADS - 1))
                if heads[-1] == HEADS - 1:
                    last.then_inc(attn_done, 1)

            def turn_attn(group, into):
                pe.wait_ge(attn_copied, group + 1)
                for k in range(2):
                    last = nc.tensor.transpose(into[:, k * P:(k + 1) * P], attn_t[:, k * P:(k + 1) * P], ident[:])
                last.then_inc(attn_turned, 1)

            gate_bank, up_bank, spread_bank, misc = bank[0:2], bank[2:4], bank[4:6], bank[6]

            def turn_x2(quad, into):
                pe.wait_ge(xn2_made, quad + 1)
                for k in range(4):
                    last = nc.tensor.transpose(into[:, k * P:(k + 1) * P], xn2[:, k, :], ident[:])
                last.then_inc(x2t_done, 1)

            def logits(quad, into):
                pe.wait_ge(x2_f_made, quad + 1)
                for k in range(4):
                    last = nc.tensor.matmul(into[:, k * EXPERTS:(k + 1) * EXPERTS], x2_f[:, k * P:(k + 1) * P],
                                            gw_t[:], start=True, stop=True)
                last.then_inc(logit_done, 1)

            def turn_route(quad, into):
                pe.wait_ge(route_made, quad + 1)
                at_least(pe, out_made, quad - 1)
                for k in range(4):
                    last = nc.tensor.transpose(into[0:2 * EXPERTS, k * P:(k + 1) * P],
                                               route2[:, k, :].bitcast(F32), ident[:])
                last.then_inc(route_turned, 1)

            pe.wait_ge(mask_made, 2)
            turn_ctx(0, 0, 0)
            turn_x(0, rot[0])
            pe.wait_ge(ct_lo_made, 1)
            for j in range(8):
                if j == 0:
                    pe.wait_ge(mask_made, 3)
                if j == 1:
                    pe.wait_ge(xt_copied, 1)
                if j % 4 == 0:
                    pe.wait_ge(m_lo_made, j // 2 + 2)
                at_least(pe, keys_copied, j - 2)
                project_keys(j, rot[(j + 2) % 3])
            pe.wait_ge(small_in, 32)
            nc.tensor.transpose(score_bank[1][:, 0:EXPERTS], gw_row[:], ident[0:EXPERTS, 0:EXPERTS]
                                ).then_inc(gwt_done, 1)
            pe.wait_ge(keys_copied, 6)
            turn_ctx(1, 1, 0)
            pe.wait_ge(wo_in, 16)
            for c in range(2):
                pe.wait_ge(m_lo_made, 2 + c)
                for n in range(4):
                    k = 4 * c + n
                    last = nc.tensor.transpose(pv_bank[c][:, n * P:(n + 1) * P], wo_s[:, k * P:(k + 1) * P],
                                               ident[:])
                last.then_inc(wot_done, 1)
            pe.wait_ge(keys_copied, 8)
            pe.wait_ge(mask_made, 4)
            pe.wait_ge(gwt_copied, 1)
            scores(0, 0)
            pe.wait_ge(ct_lo_made, 2)
            project_keys(0, rot[1])
            project_keys(1, rot[2])
            project_keys(2, rot[0])
            pe.wait_ge(keys_copied, 9)
            project_keys(3, rot[1])
            pe.wait_ge(wv_in, 16)
            pe.wait_ge(wot_copied, 2)
            for c in range(4):
                if c == 3:
                    pe.wait_ge(keys_copied, 10)
                for k, h in enumerate(heads_of(c)):
                    last = nc.tensor.matmul(b_bank[c][:, k * P:(k + 1) * P], of_head(wv_s, h),
                                            of_head(wo_t, h), start=True, stop=True)
                last.then_inc(b_done, 1)

            def body(i, first, last):
                for s in range(4):
                    pair, parity, r = 4 * i + s, s // 2, s % 2
                    group = 2 * i + parity
                    last_group = last and parity == 1
                    if not (last and s == 3):
                        if r == 0:
                            at_least(pe, keys_copied, 8 * group + 8)
                        else:
                            pe.wait_ge(xt_copied, group + 2)
                            pe.wait_ge(keys_copied, 8 * (group + 1) + 8)
                        scores(pair + 1, (s + 1) % 4)
                    at_least(pe, pt_lo_made, 2 * pair)
                    if r == 0:
                        if not last_group:
                            pe.wait_ge(keys_copied, 8 * (group + 1) + 3)
                        turn_probs(pair, 0, rot[0])
                        if not last_group:
                            pe.wait_ge(keys_copied, 8 * (group + 1) + 4)
                        turn_probs(pair, 1, rot[1])
                    else:
                        if not last_group:
                            pe.wait_ge(keys_copied, 8 * (group + 1) + 8)
                        else:
                            at_least(pe, x2_made, group - 2)
                        turn_probs(pair, 0, rot[2])
                        if not last_group:
                            pe.wait_ge(xt_copied, group + 2)
                        turn_probs(pair, 1, rot[0])
                    after_first = not (first and parity == 0)
                    if after_first:
                        if r == 0:
                            pe.wait_ge(r_lo_made, 8 * group)
                            at_least(pe, attn_copied, group - 1)
                        add_heads(group - 1, 1 - parity, range(8 * r, 8 * r + 4))
                    if first and s == 0:
                        pe.wait_ge(b_lo_made, 4)
                    if r == 0 and not last_group:
                        project_keys(4, rot[2])
                        pe.wait_ge(pt_lo_made, 2 * pair + 1)
                        project_keys(5, rot[0])
                    if r == 1 and not last:
                        pe.wait_ge(ct_lo_made, group + 3)
                        project_keys(0, rot[1])
                        pe.wait_ge(pt_lo_made, 2 * pair + 1)
                        project_keys(1, rot[2])
                    pe.wait_ge(pt_lo_made, 2 * pair + 2)
                    if r == 0:
                        pe.wait_ge(ctx_lo_made, group + 1)
                    probs_by_ctx(pair, s, 0)
                    if last and s == 3:
                        turn_x2(0, rot[1])
                    if r == 0 and not last_group:
                        project_keys(6, rot[1])
                        pe.wait_ge(keys_copied, 8 * (group + 1) + 5)
                        project_keys(7, rot[2])
                        pe.wait_ge(keys_copied, 8 * (group + 1) + 6)
                        turn_x(group + 1, rot[0])
                    if r == 1 and not last:
                        project_keys(2, rot[0])
                        pe.wait_ge(keys_copied, 8 * (group + 2) + 1)
                        project_keys(3, rot[1])
                    if r == 1 and not first:
                        pe.wait_ge(keys_copied, 8 * (group + 2) + 2) if not last else pe.wait_ge(pt_lo_made, 2 * pair + 1)
                        turn_attn(group - 2, rot[2])
                    if after_first:
                        add_heads(group - 1, 1 - parity, range(8 * r + 4, 8 * r + 8))
                    if last and s == 3:
                        pe.wait_ge(masked, 2 * PAIRS)
                        logits(0, score_bank[0])
                    probs_by_ctx(pair, s, 1)
                    if r == 0 and not last:
                        pe.wait_ge(keys_copied, 8 * (group + 1) + 7)
                        turn_ctx(group + 2, parity, i + 1)

            body(0, True, False)
            with pe.Fori(1, BODIES - 1) as i:
                body(i, False, False)
            body(BODIES - 1, False, True)
            pe.wait_ge(x2_f_made, 1)
            turn_attn(GROUPS - 2, rot[1])

            def rest_of_attention():
                pe.wait_ge(r_lo_made, 4 * PAIRS)
                pe.wait_ge(attn_copied, GROUPS - 1)
                add_heads(GROUPS - 1, 1, range(HEADS))

            def up(quad, n):
                hi = x2_hi[:, bass.ds(quad, 1), :].rearrange("p a t -> p (a t)")
                lo = x2_lo[:, bass.ds(quad, 1), :].rearrange("p a t -> p (a t)")
                q = n % 2
                step_no = BLOCKS * quad + n
                if n < BLOCKS - 1:
                    at_least(pe, prod_made, step_no - 1 if n > 1 else step_no - 2)
                if isinstance(quad, int) and quad == 0 and n == 1:
                    pe.wait_ge(x2_made, GROUPS - 1)
                if n == BLOCKS - 1:
                    at_least(pe, hid_made, 8 * quad + n - 1)
                    three(spread_bank[q][:], wg_hi[:, n, :], wg_lo[:, n, :], hi, lo).then_inc(gate_done, 1)
                    return
                three(gate_bank[q][:], wg_hi[:, n, :], wg_lo[:, n, :], hi, lo).then_inc(gate_done, 1)
                if isinstance(quad, int) and quad == 0 and n < 2:
                    pe.wait_ge(x2_made, GROUPS - 2) if n == 0 else pe.wait_ge(logit_made, 1)
                at_least(pe, hid_made, 8 * quad + n - 1)
                three(up_bank[q][:], wu_hi[:, n, :], wu_lo[:, n, :], hi, lo)

            def spread(quad, n):
                q = n % 2
                if n == 0:
                    pe.wait_ge(route_copied, quad + 1)
                    pe.wait_ge(sel_made, 1)
                    at_least(pe, prod_made, BLOCKS * quad)
                nc.tensor.matmul(spread_bank[q][:], sel[:, n, :], route_t, start=True, stop=True
                                 ).then_inc(up_done, 1)

            def down(quad, n):
                rows = P if n < BLOCKS - 1 else MID
                if n == 0:
                    at_least(pe, y_copied, quad)
                    if isinstance(quad, int) and quad == 0:
                        pe.wait_ge(x2_made, GROUPS)
                        pe.wait_ge(ffn_lo_made, 4)
                pe.wait_ge(hid_lo_made, BLOCKS * quad + n + 1)
                last = three(acc[:], wd_hi[0:rows, n, :], wd_lo[0:rows, n, :], hid_hi[0:rows, place(n)],
                             hid_lo[0:rows, place(n)], start=(n == 0), stop=(n == BLOCKS - 1))
                if n == BLOCKS - 1:
                    last.then_inc(y_done, 1)

            def quad_body(quad, first, last):
                for n in range(BLOCKS):
                    if n == 0:
                        pe.wait_ge(x2_lo_made, quad + 1)
                    if first and n == 1:
                        spread(quad, n)
                        continue_first(quad)
                        continue
                    up(quad, n)
                    if first and n == 0:
                        rest_of_attention()
                        up(quad, 1)
                        turn_route(0, score_bank[1])
                    elif n == 0:
                        turn_route(quad, misc)
                    elif n < BLOCKS - 1:
                        spread(quad, n)
                    if n >= LAG:
                        down(quad, n - LAG)
                    elif not first:
                        down(quad - 1, BLOCKS - LAG + n)
                    if n == 0:
                        spread(quad, n)
                    if n == 1 and not last:
                        turn_x2(quad + 1, misc)
                    if n == 2 and not last:
                        logits(quad + 1, misc)
                    if n == 5 and not first:
                        turn_y(quad - 1, last)

            def continue_first(quad):
                pe.wait_ge(r_lo_made, 4 * PAIRS)
                turn_x2(quad + 1, misc)
                turn_attn(GROUPS - 1, acc[:, GT:2 * GT])

            def turn_y(quad, last):
                pe.wait_ge(y_copied, quad + 1)
                if not last:
                    pe.wait_ge(logit_made, quad + 3)
                for k in range(4):
                    ins = nc.tensor.transpose(misc[:, k * P:(k + 1) * P], y_t[:, k * P:(k + 1) * P], ident[:])
                ins.then_inc(y_turned, 1)

            pe.wait_ge(ffn_lo_made, 2)
            pe.wait_ge(pt_lo_made, 2 * PAIRS)
            quad_body(0, True, False)
            with pe.Fori(1, QUADS - 1) as quad:
                quad_body(quad, False, False)
            quad_body(QUADS - 1, False, True)
            for n in range(BLOCKS - LAG, BLOCKS):
                down(QUADS - 1, n)
            pe.wait_ge(out_made, QUADS - 1)
            turn_y(QUADS - 1, True)

        @block.scalar
        def _(act):
            copy = lambda dst, src: nc.scalar.activation(dst, src, ACT.Copy)

            act.dma_start(mask_u8[:], mask.rearrange("(t b) k -> b t k", b=2)).then_inc(mask_in, 16)
            act.dma_start(xall[:, 0:4, :], x_tiles[:, 0:4, :]).then_inc(x_first_in, 16)
            for c in range(4):
                act.wait_ge(m_done, c + 1)
                copy(four_heads(m_hi, c), by_two(bank[4 + c][:])).then_inc(m_hi_made, 1)

            def b_high(c):
                act.wait_ge(b_done, c + 1)
                copy(four_heads(b_hi, c), by_two(b_bank[c][:])).then_inc(b_hi_made, 1)

            def ctx_t_high(group):
                act.wait_ge(ct_done, group + 1)
                copy(ct_hi[:].rearrange("p (b k) -> p b k", k=SEQ), once(rot[1])).then_inc(ct_hi_made, 1)

            def x_t(group, parity, src):
                act.wait_ge(xt_done, group + 1)
                at_least(act, scores_done, 4 * (group - 1))
                copy(xt[:, parity, :], src[:, 0:GT]).then_inc(xt_copied, 1)

            def keys_out(group, parity, j, src):
                act.wait_ge(keys_done, 8 * group + j + 1)
                if j == 0:
                    at_least(act, scores_done, 4 * (group - 1))
                copy(keys[:, parity, 2 * j:2 * j + 2, :].rearrange("p h t -> p (h t)"), src[:]
                     ).then_inc(keys_copied, 1)

            def exponentials(pair, half):
                act.wait_ge(shifted, 2 * pair + half + 1)
                part = probs[:, 8 * half:8 * half + 8, :]
                nc.scalar.activation(part, part, ACT.Exp, scale=HD ** -0.5).then_inc(exp_made, 1)

            def probs_t_high(pair, v, src):
                act.wait_ge(pt_done, 2 * pair + v + 1)
                if v == 0:
                    at_least(act, pv_done, 4 * pair)
                copy(pt_hi[:, 4 * v:4 * v + 4, :].rearrange("p h q -> p (h q)"), src[:]).then_inc(pt_hi_made, 1)

            def r_high(pair, s, b):
                parity, r = s // 2, s % 2
                for h2 in range(2):
                    act.wait_ge(pv_done, 4 * pair + 2 * b + h2 + 1)
                    col = r * P + b * SEQ
                    dst = r_hi[:, parity, :, col:col + SEQ].rearrange("p (n a) q -> p n a q", a=2)[:, :, h2, :]
                    copy(dst, pv_bank[h2][:].rearrange("p (n q) -> p n q", q=SEQ)).then_inc(r_hi_made, 1)

            def attn_out(group):
                act.wait_ge(attn_done, group + 1)
                at_least(act, attn_turned, group)
                nc.scalar.activation(attn_t[:], acc[:, 0:GT], ACT.Identity, bias=bo_col[:, 0:1]
                                     ).then_inc(attn_copied, 1)

            ctx_t_high(0)
            x_t(0, 0, rot[0])
            for j in range(8):
                keys_out(0, 0, j, rot[(j + 2) % 3])
            misc = bank[6]
            act.wait_ge(gwt_done, 1)
            copy(gw_t[:], score_bank[1][:, 0:EXPERTS]).then_inc(gwt_copied, 1)
            ctx_t_high(1)
            for c in range(2):
                act.wait_ge(wot_done, c + 1)
                copy(wo_t[:, 4 * c:4 * c + 4, :].rearrange("p n e -> p (n e)"), pv_bank[c][:]).then_inc(wot_copied, 1)
            for j in range(4):
                keys_out(1, 1, j, rot[(j + 1) % 3])
                if j >= 2:
                    exponentials(0, j - 2)
            for c in range(4):
                b_high(c)
            act.wait_ge(small_in, 32)

            def x2_high(quad, src):
                act.wait_ge(x2t_done, quad + 1)
                copy(x2_hi[:, bass.ds(quad, 1), :].rearrange("p a t -> p (a t)"), src[:])
                copy(x2_f, src[:]).then_inc(x2_f_made, 1)

            def weight_high(k):
                hi, lo, raw = ffn_parts[k]
                act.wait_ge(ffn_in, 16 * 6)
                copy(hi, raw).then_inc(ffn_hi_made, 1)

            def body(i, first, last):
                for s in range(4):
                    pair, parity, r = 4 * i + s, s // 2, s % 2
                    group = 2 * i + parity
                    last_group = last and parity == 1
                    if r == 0 and not first:
                        attn_out(group - 2)
                    turned = (rot[0], rot[1]) if r == 0 else (rot[2], rot[0])
                    probs_t_high(pair, 0, turned[0])
                    probs_t_high(pair, 1, turned[1])
                    have_keys = not last_group if r == 0 else not last
                    key_args = ([(group + 1, 1 - parity, 4 + j, rot[(j + 2) % 3]) for j in range(4)] if r == 0 else
                                [(group + 2, parity, j, rot[(j + 1) % 3]) for j in range(4)])
                    for j in range(4):
                        if j == 2:
                            if last and s == 2:
                                weight_high(0)
                            if last and s == 3:
                                weight_high(1)
                            r_high(pair, s, 0)
                            if not (last and s == 3):
                                exponentials(pair + 1, 0)
                                exponentials(pair + 1, 1)
                        if have_keys:
                            keys_out(*key_args[j])
                    if r == 0 and not last_group:
                        x_t(group + 1, 1 - parity, rot[0])
                    if last and s == 3:
                        x2_high(0, rot[1])
                        attn_out(GROUPS - 2)
                    r_high(pair, s, 1)
                    if r == 0 and not last:
                        ctx_t_high(group + 2)

            body(0, True, False)
            with act.Fori(1, BODIES - 1) as i:
                body(i, False, False)
            body(BODIES - 1, False, True)

            gate_bank, spread_bank = bank[0:2], bank[4:6]

            def logit_silus(quad):
                act.wait_ge(logit_made, quad + 1)
                nc.scalar.activation(logit_silu[:], logit[:], ACT.Silu).then_inc(silu_of_logit, 1)

            def route_out(quad, src):
                act.wait_ge(route_turned, quad + 1)
                copy(route_t, src[0:2 * EXPERTS, :]).then_inc(route_copied, 1)

            def silu(quad, n):
                step_no = BLOCKS * quad + n
                rows = P if n < BLOCKS - 1 else MID
                act.wait_ge(gate_done, step_no + 1)
                at_least(act, prod_made, step_no - 2)
                src = gate_bank[n % 2] if n < BLOCKS - 1 else spread_bank[0]
                nc.scalar.activation(sg[0:rows, n % 3], src[0:rows, :], ACT.Silu
                                     ).then_inc(silu_made, 1)

            def hid_high(quad, n):
                step_no = BLOCKS * quad + n
                if n < BLOCKS - 1:
                    rows = P
                    act.wait_ge(hid_made, 8 * quad + n + 1)
                else:
                    rows = MID
                    act.wait_ge(prod_made, step_no + 1)
                copy(hid_hi[0:rows, place(n)], hid[0:rows, place(n)]).then_inc(hid_hi_made, 1)

            def y_out(quad):
                act.wait_ge(y_done, quad + 1)
                copy(y_t, acc[:]).then_inc(y_copied, 1)

            def quad_body(quad, first, last):
                for n in range(BLOCKS):
                    if n == LAG and not first:
                        y_out(quad - 1)
                    silu(quad, n)
                    if first and n == 0:
                        attn_out(GROUPS - 1)
                        route_out(0, score_bank[1])
                    elif n == 0:
                        route_out(quad, misc)
                    if n == 1 and not last:
                        x2_high(quad + 1, misc)
                    if n > 0:
                        hid_high(quad, n - 1)
                    elif not first:
                        hid_high(quad - 1, BLOCKS - 1)
                    if n == 3 and not last:
                        logit_silus(quad + 1)

            act.wait_ge(pv_done, 4 * PAIRS)
            act.wait_ge(sel_f_made, 1)
            copy(sel, sel_f).then_inc(sel_made, 1)
            weight_high(2)
            weight_high(3)
            logit_silus(0)
            quad_body(0, True, False)
            with act.Fori(1, QUADS - 1) as quad:
                quad_body(quad, False, False)
            quad_body(QUADS - 1, False, True)
            hid_high(QUADS - 1, BLOCKS - 1)
            y_out(QUADS - 1)

        @block.vector
        def _(dve):
            sub = lambda dst, a, b: nc.vector.tensor_tensor(dst, a, b, ALU.subtract)
            flat = lambda ap: ap.rearrange("p a b -> p (a b)")

            dve.wait_ge(mask_in, 16)
            nc.vector.tensor_scalar(mask_neg, mask_u8[:], -1.0, -MASKED, ALU.add, ALU.mult
                                    ).then_inc(mask_neg_made, 1)

            def wait_before(sem_, value):
                dve.wait_ge(sem_, value)
                nc.vector.memset(wait_cell[:], 0.0)

            def statistics(group):
                for k in range(2):
                    tile = flat(xall[:, bass.ds(2 * group + k, 1), :])
                    last = nc.vector.bn_stats(stats[:, k, :], tile)
                last.then_inc(ln_step, 1)
                at_least(dve, xn_made, group)
                wait_before(ln_step, 2 * group + 1)
                for k in range(2):
                    last = nc.vector.bn_aggr(mean_var[:, k, :], stats[:, k, :])
                last.then_inc(ln_step, 1)
                dve.wait_ge(ln_step, 2 * group + 2)
                nc.vector.tensor_scalar(var_eps[:, 0:2, :], mean_var[:, 0:2, 1:2], LN_EPS, None, ALU.add
                                        ).then_inc(var_made, 1)

            def m_low(c):
                dve.wait_ge(m_hi_made, c + 1)
                sub(four_heads(m_lo, c), by_two(bank[4 + c][:]), four_heads(m_hi, c)).then_inc(m_lo_made, 1)

            def b_low(c):
                dve.wait_ge(b_hi_made, c + 1)
                sub(four_heads(b_lo, c), by_two(b_bank[c][:]), four_heads(b_hi, c)).then_inc(b_lo_made, 1)

            dve.wait_ge(x_first_in, 16)
            statistics(0)
            dve.wait_ge(consts_made, 4)
            for c in range(4):
                dve.wait_ge(mask_spread, c + 1)
                nc.vector.tensor_tensor(maskb[:, 8 * c:8 * c + 8, :],
                                        bank[c][:].rearrange("p (t k) -> p t k", k=SEQ),
                                        tri[:].unsqueeze(1).to_broadcast([P, 8, SEQ]), ALU.add
                                        ).then_inc(mask_made, 1)

            def ctx_t_low(group):
                dve.wait_ge(ct_hi_made, group + 1)
                sub(ct_lo[:].rearrange("p (b k) -> p b k", k=SEQ), once(rot[1]),
                    ct_hi[:].rearrange("p (b k) -> p b k", k=SEQ)).then_inc(ct_lo_made, 1)

            def mask_scores(pair, half):
                dve.wait_ge(scores_done, 2 * pair + half + 1)
                if half == 0:
                    at_least(dve, pt_done, 2 * pair)
                nc.vector.tensor_tensor(probs[:, 8 * half:8 * half + 8, :],
                                        score_bank[half][:].rearrange("p (h k) -> p h k", k=SEQ),
                                        maskb[:, bass.ds(pair, 1), :].to_broadcast([P, 8, SEQ]), ALU.add
                                        ).then_inc(masked, 1)

            def maximum(pair, half):
                heads = slice(8 * half, 8 * half + 8)
                dve.wait_ge(masked, 2 * pair + half + 1)
                nc.vector.tensor_reduce(row_max[:, heads], probs[:, heads, :], AX_X, ALU.max).then_inc(max_made, 1)

            def sums(pair):
                for half in range(2):
                    heads = slice(8 * half, 8 * half + 8)
                    dve.wait_ge(exp_made, 2 * pair + half + 1)
                    nc.vector.tensor_reduce(row_sum[:, heads], probs[:, heads, :], AX_X, ALU.add
                                            ).then_inc(sum_made, 1)
                nc.vector.tensor_scalar(nan_probe[:], row_max[:], 1e9, None, ALU.mult).then_inc(inv_step, 1)
                dve.wait_ge(sum_made, 2 * pair + 2)
                nc.vector.reciprocal(inv_raw[:], row_sum[:]).then_inc(inv_step, 1)
                dve.wait_ge(inv_step, 2 * pair + 2)
                at_least(dve, probs_made, 2 * pair)
                nc.vector.scalar_tensor_tensor(inv[:], nan_probe[:], 0.0, inv_raw[:], ALU.mult, ALU.add
                                               ).then_inc(inv_made, 1)

            def shift(pair):
                for half in range(2):
                    heads = slice(8 * half, 8 * half + 8)
                    dve.wait_ge(max_made, 2 * pair + half + 1)
                    sub(probs[:, heads, :], probs[:, heads, :],
                        row_max[:, heads].unsqueeze(2).to_broadcast([P, 8, SEQ])).then_inc(shifted, 1)

            def normalise(pair):
                dve.wait_ge(inv_made, pair + 1)
                for half in range(2):
                    heads = slice(8 * half, 8 * half + 8)
                    nc.vector.tensor_tensor(probs[:, heads, :], probs[:, heads, :],
                                            inv[:, heads].unsqueeze(2).to_broadcast([P, 8, SEQ]),
                                            ALU.mult).then_inc(probs_made, 1)

            def probs_t_low(pair, v, src):
                dve.wait_ge(pt_hi_made, 2 * pair + v + 1)
                part = slice(4 * v, 4 * v + 4)
                sub(flat(pt_lo[:, part, :]), src[:], flat(pt_hi[:, part, :])).then_inc(pt_lo_made, 1)

            def r_low(pair, s, b):
                parity, r = s // 2, s % 2
                col = r * P + b * SEQ
                for h2 in range(2):
                    dve.wait_ge(r_hi_made, 4 * pair + 2 * b + h2 + 1)
                    pick = lambda t: t[:, parity, :, col:col + SEQ].rearrange("p (n a) q -> p n a q", a=2)[:, :, h2, :]
                    sub(pick(r_lo), pv_bank[h2][:].rearrange("p (n q) -> p n q", q=SEQ), pick(r_hi)
                        ).then_inc(r_lo_made, 1)

            def add_attn(group, src):
                dve.wait_ge(attn_turned, group + 1)
                tiles = xall[:, bass.ds(2 * group, 2), :]
                nc.vector.tensor_tensor(tiles, src[:, 0:GT].rearrange("p (t d) -> p t d", d=P), tiles, ALU.add
                                        ).then_inc(x2_made, 1)

            def statistics2(group):
                wait_before(x2_made, group + 1)
                for k in range(2):
                    last = nc.vector.bn_stats(stats2[:, k, :], flat(xall[:, bass.ds(2 * group + k, 1), :]))
                last.then_inc(ln2_step, 1)
                wait_before(ln2_step, 2 * group + 1)
                for k in range(2):
                    last = nc.vector.bn_aggr(mean_var2[:, k, :], stats2[:, k, :])
                last.then_inc(ln2_step, 1)
                dve.wait_ge(ln2_step, 2 * group + 2)
                nc.vector.tensor_copy(moments2[:, bass.ds(2 * group, 2), :], mean_var2[:]).then_inc(var2_made, 1)

            def layer_norm2(quad):
                at_least(dve, x2t_done, quad)
                for k in range(4):
                    last = nc.vector.tensor_scalar(xn2[:, k, :], flat(xall[:, bass.ds(4 * quad + k, 1), :]),
                                                   flat(moments2[:, bass.ds(4 * quad + k, 1), 0:1]),
                                                   flat(rstd2[:, bass.ds(4 * quad + k, 1), :]),
                                                   ALU.subtract, ALU.mult)
                last.then_inc(xn2_made, 1)

            m_low(0)
            m_low(1)
            ctx_t_low(0)
            m_low(2)
            m_low(3)
            statistics(1)
            ctx_t_low(1)
            for half in range(2):
                mask_scores(0, half)
                maximum(0, half)
            sums(0)
            for c in range(4):
                b_low(c)
            dve.wait_ge(x_rest_in, 16)

            def body(i, first, last):
                for s in range(4):
                    pair, parity, r = 4 * i + s, s // 2, s % 2
                    group = 2 * i + parity
                    more = not (last and s == 3)
                    turned = (rot[0], rot[1]) if r == 0 else (rot[2], rot[0])
                    probs_t_low(pair, 0, turned[0])
                    if more:
                        mask_scores(pair + 1, 0)
                    probs_t_low(pair, 1, turned[1])
                    if more:
                        mask_scores(pair + 1, 1)
                    if last and s == 3:
                        dve.wait_ge(pt_done, 2 * PAIRS)
                        dve.wait_ge(rstd2_made, 1)
                        layer_norm2(0)
                    if more:
                        maximum(pair + 1, 0)
                        maximum(pair + 1, 1)
                    if last and s in (1, 2):
                        shift(pair + 1)
                    r_low(pair, s, 0)
                    if more:
                        sums(pair + 1)
                    if last and s in (1, 2):
                        normalise(pair + 1)
                    if r == 1 and not first:
                        add_attn(group - 2, rot[2])
                    r_low(pair, s, 1)
                    if r == 0 and not last:
                        ctx_t_low(group + 2)
                        statistics(group + 2)
                    if r == 1 and not first and not last:
                        statistics2(group - 2)

            body(0, True, False)
            dve.wait_ge(x_late_in, 16)
            with dve.Fori(1, BODIES - 1) as i:
                body(i, False, False)
            body(BODIES - 1, False, True)

            up_bank, spread_bank, misc = bank[2:4], bank[4:6], bank[6]
            dve.wait_ge(fill_made, 4)

            def fix_logits(quad, src):
                z = src[:, 0:4 * EXPERTS].rearrange("p (t e) -> p t e", e=EXPERTS)
                dve.wait_ge(logit_done, quad + 1)
                nc.vector.tensor_scalar(logit_fix[:], z, 0.0, 1e-20, ALU.is_equal, ALU.mult).then_inc(logit_step, 1)
                dve.wait_ge(logit_step, 2 * quad + 1)
                at_least(dve, silu_of_logit, quad)
                nc.vector.scalar_tensor_tensor(logit[:], z, SATURATED, logit_fix[:], ALU.min, ALU.add
                                               ).then_inc(logit_made, 1)
                dve.wait_ge(logit_made, quad + 1)
                nc.vector.reciprocal(logit_inv[:], logit[:]).then_inc(logit_step, 1)

            def pick_experts(quad):
                t0 = 8 * quad
                dve.wait_ge(silu_of_logit, quad + 1)
                dve.wait_ge(logit_step, 2 * quad + 2)
                real = score[:, :, 0:EXPERTS]
                nc.vector.tensor_tensor(real, logit_silu[:], logit_inv[:], ALU.mult).then_inc(top_step, 1)
                wait_before(top_step, t0 + 1)
                for k in range(4):
                    last = nc.vector.max(best[:, k, :], score[:, k, :])
                last.then_inc(top_step, 1)
                dve.wait_ge(top_step, t0 + 2)
                nc.vector.tensor_copy(taken[:, :, 0:2], best[:, :, 0:2]).then_inc(top_step, 1)
                nc.vector.tensor_tensor(best_sum[:], best[:, :, 0:1], best[:, :, 1:2], ALU.add).then_inc(top_step, 1)

            def mark_experts(quad):
                t0 = 8 * quad
                real = score[:, :, 0:EXPERTS]
                wait_before(top_step, t0 + 4)
                for k in range(4):
                    last = nc.vector.match_replace(marked[:, k, :], taken[:, k, :], score[:, k, :], -5.0)
                last.then_inc(top_step, 1)
                nc.vector.tensor_scalar(best_sum[:], best_sum[:], 1e-20, None, ALU.add).then_inc(top_step, 1)
                dve.wait_ge(top_step, t0 + 6)
                nc.vector.reciprocal(best_inv[:], best_sum[:]).then_inc(top_step, 1)
                nc.vector.scalar_tensor_tensor(picked[:], marked[:, :, 0:EXPERTS], -3.0, real, ALU.is_lt, ALU.mult
                                               ).then_inc(top_step, 1)
                dve.wait_ge(top_step, t0 + 8)

            def split_route(quad):
                nc.vector.scalar_tensor_tensor(route[:], picked[:], TOP_SCALE,
                                               best_inv[:].to_broadcast([P, 4, EXPERTS]), ALU.mult, ALU.mult
                                               ).then_inc(route_step, 1)
                dve.wait_ge(route_step, 2 * quad + 1)
                at_least(dve, route_turned, quad)
                nc.vector.tensor_copy(route2[:, :, 0:EXPERTS], route[:]).then_inc(route_step, 1)
                dve.wait_ge(route_step, 2 * quad + 2)
                sub(route2[:, :, EXPERTS:2 * EXPERTS], route[:], route2[:, :, 0:EXPERTS]).then_inc(route_made, 1)

            def product(quad, n):
                step_no = BLOCKS * quad + n
                dve.wait_ge(silu_made, step_no + 1)
                at_least(dve, hid_lo_made, step_no - 3)
                if n < BLOCKS - 1:
                    dve.wait_ge(up_done, 8 * quad + n + 1)
                    nc.vector.tensor_tensor(hid[:, place(n)], up_bank[n % 2][:], sg[:, n % 3], ALU.mult
                                            ).then_inc(prod_made, 1)
                    dve.wait_ge(prod_made, step_no + 1)
                    nc.vector.tensor_tensor(hid[:, place(n)], spread_bank[n % 2][:], hid[:, place(n)], ALU.mult
                                            ).then_inc(hid_made, 1)
                else:
                    nc.vector.tensor_tensor(hid[0:MID, place(n)], spread_bank[0][MID:P, :], sg[0:MID, n % 3], ALU.mult
                                            ).then_inc(prod_made, 1)

            def add_experts(quad):
                dve.wait_ge(y_turned, quad + 1)
                at_least(dve, out_stored, 16 * quad)
                nc.vector.tensor_tensor(out_sb, misc[:].rearrange("p (t d) -> p t d", d=P),
                                        xall[:, bass.ds(4 * quad, 4), :], ALU.add).then_inc(out_made, 1)

            def hid_low(quad, n):
                rows = P if n < BLOCKS - 1 else MID
                step_no, at = BLOCKS * quad + n, place(n)
                dve.wait_ge(hid_hi_made, step_no + 1)
                dve.wait_ge(hid_lo_made, step_no)
                sub(hid_lo[0:rows, at], hid[0:rows, at], hid_hi[0:rows, at]).then_inc(hid_lo_made, 1)

            def quad_body(quad, first, last):
                for n in range(BLOCKS):
                    if n == 0 and not last:
                        layer_norm2(quad + 1)
                    product(quad, n)
                    if last and n > BLOCKS - LAG:
                        hid_low(quad, n - 1)
                    if first and n == 1:
                        add_attn(GROUPS - 1, acc[:, GT:2 * GT])
                    if first and n in (2, 3, 4, 5):
                        statistics2(GROUPS - 6 + n)
                    if n == 3 and not last:
                        fix_logits(quad + 1, misc)
                    if n == 4 and not last:
                        pick_experts(quad + 1)
                    if n == 6 and not last:
                        mark_experts(quad + 1)
                    if n == 7 and not last:
                        split_route(quad + 1)
                    if n == 5 and not first:
                        add_experts(quad - 1)

            fix_logits(0, score_bank[0])
            pick_experts(0)
            add_attn(GROUPS - 2, rot[1])
            mark_experts(0)
            split_route(0)
            quad_body(0, True, False)
            dve.wait_ge(rstd2_made, 2)
            with dve.Fori(1, QUADS - 1) as quad:
                quad_body(quad, False, False)
            quad_body(QUADS - 1, False, True)
            hid_low(QUADS - 1, BLOCKS - 1)
            add_experts(QUADS - 1)


_INS = ['x', 'ctx_1024', 'mask_BxS2_bf1', 'L0_xattn_Wq', 'L0_xattn_Wk', 'L0_xattn_Wv', 'L0_xattn_Wo', 'L0_xattn_bo',
        'L0_ffn_gate_w', 'L0_ffn_w_gate', 'L0_ffn_w_up', 'L0_ffn_w_down', 'L0_ffn_ws_gate', 'L0_ffn_ws_up',
        'L0_ffn_ws_down']


def kernel(**inputs):
    import numpy as _np
    import concourse.bacc as _bacc
    from concourse import mybir as _mybir
    from concourse.bass_utils import run_bass_kernel_spmd as _run

    nc = _bacc.Bacc("TRN2", target_bir_lowering=False, num_devices=1)
    arrays, args = {}, []
    for name in _INS:
        a = _np.ascontiguousarray(inputs[name])
        if a.dtype == _np.bool_:
            a = a.view(_np.uint8)
        arrays[f"in_{name}"] = a
        args.append(nc.dram_tensor(f"in_{name}", a.shape, _mybir.dt.from_np(a.dtype), kind="ExternalInput").ap())
    shape = inputs['x'].shape
    args.append(nc.dram_tensor("out_x", tuple(shape), _mybir.dt.float32, kind="ExternalOutput").ap())
    xattn_moe_kernel(nc, *args)
    r = _run(nc, [arrays], core_ids=[0])
    return r.results[0]["out_x"]
```
